# Optimizing a Trainium2 kernel written in Bass

```python
import numpy as np
import jax
import jax.numpy as jnp

def _softmax(x, axis=-1):
    return jax.nn.softmax(x, axis=axis)

def _gelu(x):
    return jax.nn.gelu(x, approximate=True)

def _silu(x):
    return jax.nn.silu(x)

def _sigmoid(x):
    return jax.nn.sigmoid(x)

def _layernorm(x, axis=-1, eps=1e-05):
    m = jnp.mean(x, axis=axis, keepdims=True)
    v = jnp.var(x, axis=axis, keepdims=True)
    return (x - m) / jnp.sqrt(v + eps)

def _scatter_add(tgt, idx, src, axis=0):
    return tgt.at[idx].add(src)

def _segment_sum(src, seg, n):
    return jax.ops.segment_sum(src, seg, n)
kernel_name = 'mk_adaln_ffn_d1_seqx_r8_fa1f01'

def setup_inputs(seed: int=0):
    np.random.seed(seed)
    _w = jnp.asarray

    def _rec_inputs():
        import jax
        import jax.numpy as jnp
        _rk = jax.random.key(seed)
        x = -0.000125 + 0.9999 * jax.random.normal(jax.random.fold_in(_rk, 1), (128, 32, 512), jnp.float32)
        _lenS = 32 - jax.random.randint(jax.random.fold_in(_rk, 7), (128,), 0, max(1, 32 // 4) + 1, jnp.int32)
        _lenS2 = 32 - jax.random.randint(jax.random.fold_in(_rk, 8), (128,), 0, max(1, 32 // 4) + 1, jnp.int32)
        cond_128 = 0.0061147 + 1.02565 * jax.random.normal(jax.random.fold_in(_rk, 11), (128, 128), jnp.float32)
        return (x, cond_128)
    x, cond_128 = _rec_inputs()

    def _L0_cond_setup():
        import jax, jax.numpy as jnp
        import numpy as np
        K = 8
        T = 1.0
        D_EMBD = 128
        IN_C = 32
        OUT_C = 32
        BS = 32
        H = 512
        HID = 128
        key = jax.random.key(seed)
        ks = jax.random.split(key, 10)
        s = lambda fan_in: 1.0 / np.sqrt(fan_in)
        return {'x': jax.random.normal(ks[0], (BS, IN_C, H), dtype=jnp.float32), 'embedding': jax.random.normal(ks[1], (BS, D_EMBD), dtype=jnp.float32), 'W0': jax.random.normal(ks[2], (D_EMBD, HID), dtype=jnp.float32) * s(D_EMBD), 'b0': jnp.zeros((HID,), dtype=jnp.float32), 'W1': jax.random.normal(ks[3], (HID, HID), dtype=jnp.float32) * s(HID), 'b1': jnp.zeros((HID,), dtype=jnp.float32), 'W2': jax.random.normal(ks[4], (HID, K), dtype=jnp.float32) * s(HID), 'b2': jnp.zeros((K,), dtype=jnp.float32), 'weight': jax.random.normal(ks[5], (K, OUT_C, IN_C, 1), dtype=jnp.float32) * s(IN_C), 'bias_k': jax.random.normal(ks[6], (K, OUT_C), dtype=jnp.float32) * 0.1}
    _L0_cond_all = _L0_cond_setup()
    _L0_cond_in = {k: v for k, v in _L0_cond_all.items() if k in ('W0', 'b0', 'W1', 'b1', 'W2', 'b2', 'weight', 'bias_k')}
    del _L0_cond_all

    def _L0_ffn_setup():
        import jax, jax.numpy as jnp
        import numpy as np
        E = 8
        R = 8
        DIN = 512
        DOUT = 512
        TOP_K = 2
        SCALING = 2.0

        def _moe_lora(xf, gate_W, A, B):
            gate_probs = jax.nn.softmax(xf @ gate_W.T, axis=-1)
            weights, sel = jax.lax.top_k(gate_probs, TOP_K)
            weights = weights / jnp.sum(weights, axis=-1, keepdims=True)
            T = xf.shape[0]
            w_dense = jnp.zeros((T, E), xf.dtype).at[jnp.arange(T)[:, None], sel].add(weights)
            h = jnp.einsum('td,erd->ter', xf, A)
            h = h * (w_dense[:, :, None] * SCALING)
            return jnp.einsum('ter,eor->to', h, B)
        key = jax.random.key(seed)
        k0, k1, k2, k3, k4 = jax.random.split(key, 5)
        x = jax.random.normal(k0, (4, 256, DIN), jnp.float32)
        W_base = jax.random.normal(k1, (DOUT, DIN), jnp.float32) * 0.02
        gate_W = jax.random.normal(k2, (E, DIN), jnp.float32) * 0.02
        A = jax.random.normal(k3, (E, R, DIN), jnp.float32) * 0.02
        B = jax.random.normal(k4, (E, DOUT, R), jnp.float32) * 0.02
        return {'x': x, 'W_base': W_base, 'gate_W': gate_W, 'A': A, 'B': B}
    _L0_ffn_all = _L0_ffn_setup()
    _L0_ffn_in = {k: v for k, v in _L0_ffn_all.items() if k in ('W_base', 'gate_W', 'A', 'B')}
    del _L0_ffn_all
    return {'x': x, 'cond_128': cond_128, 'L0_cond_W0': _L0_cond_in['W0'], 'L0_cond_b0': _L0_cond_in['b0'], 'L0_cond_W1': _L0_cond_in['W1'], 'L0_cond_b1': _L0_cond_in['b1'], 'L0_cond_W2': _L0_cond_in['W2'], 'L0_cond_b2': _L0_cond_in['b2'], 'L0_cond_weight': _L0_cond_in['weight'], 'L0_cond_bias_k': _L0_cond_in['bias_k'], 'L0_ffn_W_base': _L0_ffn_in['W_base'], 'L0_ffn_gate_W': _L0_ffn_in['gate_W'], 'L0_ffn_A': _L0_ffn_in['A'], 'L0_ffn_B': _L0_ffn_in['B']}

def reference(x, cond_128, L0_cond_W0, L0_cond_b0, L0_cond_W1, L0_cond_b1, L0_cond_W2, L0_cond_b2, L0_cond_weight, L0_cond_bias_k, L0_ffn_W_base, L0_ffn_gate_W, L0_ffn_A, L0_ffn_B):
    import jax
    import jax.numpy as jnp

    def _L0_cond_ref(x, embedding, W0, b0, W1, b1, W2, b2, weight, bias_k):
        import jax, jax.numpy as jnp
        import numpy as np
        K = 8
        T = 1.0
        D_EMBD = 128
        IN_C = 32
        OUT_C = 32
        BS = 32
        H = 512
        HID = 128
        h = jax.nn.gelu(embedding @ W0 + b0, approximate=False)
        h = jax.nn.gelu(h @ W1 + b1, approximate=False)
        att = jax.nn.softmax((h @ W2 + b2) / T, axis=-1)
        agg_w = jnp.einsum('bk,koi->boi', att, weight[..., 0])
        agg_b = att @ bias_k
        out = jnp.einsum('boi,bih->boh', agg_w, x) + agg_b[:, :, None]
        return out

    def _L0_ffn_ref(x, W_base, gate_W, A, B):
        import jax, jax.numpy as jnp
        import numpy as np
        E = 8
        R = 8
        DIN = 512
        DOUT = 512
        TOP_K = 2
        SCALING = 2.0

        def _moe_lora(xf, gate_W, A, B):
            gate_probs = jax.nn.softmax(xf @ gate_W.T, axis=-1)
            weights, sel = jax.lax.top_k(gate_probs, TOP_K)
            weights = weights / jnp.sum(weights, axis=-1, keepdims=True)
            T = xf.shape[0]
            w_dense = jnp.zeros((T, E), xf.dtype).at[jnp.arange(T)[:, None], sel].add(weights)
            h = jnp.einsum('td,erd->ter', xf, A)
            h = h * (w_dense[:, :, None] * SCALING)
            return jnp.einsum('ter,eor->to', h, B)
        xf = x.reshape(-1, x.shape[-1])
        out = xf @ W_base.T + _moe_lora(xf, gate_W, A, B)
        return out.reshape(*x.shape[:-1], DOUT)
    x = x + _L0_ffn_ref(_L0_cond_ref(x, cond_128, L0_cond_W0, L0_cond_b0, L0_cond_W1, L0_cond_b1, L0_cond_W2, L0_cond_b2, L0_cond_weight, L0_cond_bias_k), L0_ffn_W_base, L0_ffn_gate_W, L0_ffn_A, L0_ffn_B)
    return x

_drawn_inputs = setup_inputs


def setup_inputs(seed=0):
    import zlib

    import numpy as np

    out = dict(_drawn_inputs(seed))
    spreads = {'L0_cond_b0': (0.0, 0.8), 'L0_cond_b1': (0.0, 0.662), 'L0_cond_b2': (0.0, 0.632)}
    factors = {'L0_cond_bias_k': 3.467, 'L0_ffn_gate_W': 4.795, 'L0_ffn_A': 4.135, 'L0_ffn_B': 4.178}
    for name, (base, spread) in spreads.items():
        noise = np.random.default_rng([zlib.crc32(name.encode()), seed]).standard_normal(out[name].shape)
        drawn = base * np.exp(spread * noise) if base else spread * noise
        out[name] = jnp.asarray(drawn.astype(out[name].dtype))
    for name, factor in factors.items():
        out[name] = (out[name] * factor).astype(out[name].dtype)
    return out
```

```python
import concourse.bass as bass
from concourse import mybir
from contextlib import ExitStack


def adaln_moe_ffn_kernel(nc, x, cond, w0, b0, w1, b1, w2, b2, mix_w, mix_b, w_base, gate_w, lora_a, lora_b, out):
    f32, f32r = mybir.dt.float32, mybir.dt.float32r
    ALU = mybir.AluOpType
    ACT = mybir.ActivationFunctionType
    AX = mybir.AxisListType

    P = 128
    BATCH, CH, D = x.shape
    K = mix_w.shape[0]
    E, R, _ = lora_a.shape
    ER = E * R
    GA = ER + E
    SPT = P // CH
    TILES = BATCH // SPT
    C = D // P
    SLOTS = 4
    GROUPS = TILES // SLOTS
    QUAD = 32
    LOW = -3.0e38
    PER_ROUND = 8
    ROUNDS = CH // PER_ROUND

    x_tiles = x.rearrange("(t s) c d -> t (s c) d", s=SPT)
    out_tiles = out.rearrange("(t s) c d -> t (s c) d", s=SPT)

    ctx = ExitStack()
    with ctx:
        def sb(name, shape, dt=f32):
            return ctx.enter_context(nc.sbuf_tensor(name, shape, dt))

        def sem(name):
            return ctx.enter_context(nc.semaphore(name))

        ident = sb("ident", [P, P])
        ones = sb("ones", [P, P])
        ones_r = sb("ones_r", [P, P], f32r)
        cond_sb = sb("cond_sb", [P, P])
        condT = sb("condT", [P, P])
        w0_sb = sb("w0_sb", [P, P])
        w1_sb = sb("w1_sb", [P, P])
        w2_sb = sb("w2_sb", [P, K])
        b0_col = sb("b0_col", [P, 1])
        b1_col = sb("b1_col", [P, 1])
        b2_row = sb("b2_row", [1, K])
        h1T = sb("h1T", [P, P])
        h2T = sb("h2T", [P, P])
        att_max = sb("att_max", [P, 1])
        att_neg = sb("att_neg", [P, 1])
        att_exp = sb("att_exp", [P, K])
        att_sum = sb("att_sum", [P, 1])
        att_inv = sb("att_inv", [P, 1])
        att = sb("att", [P, K])
        att_parts = sb("att_parts", [P, 4 * QUAD])
        attT = sb("attT", [P, BATCH], f32r)
        mix_raw = sb("mix_raw", [P, CH + 1, CH])
        mix_parts = sb("mix_parts", [P, CH + 1, CH])
        mix_reps = sb("mix_reps", [P, CH + 1, SPT, CH], f32r)
        agg_bd = sb("agg_bd", [P, TILES, SPT, CH])
        agg_b = sb("agg_b", [P, TILES])
        w_nat = sb("w_nat", [P, C, D])
        wT_hi = sb("wT_hi", [P, C, D], f32r)
        wT_lo = sb("wT_lo", [P, C, D], f32r)
        ga_nat = sb("ga_nat", [GA, D])
        gaT = sb("gaT", [P, C, 2, GA], f32r)
        b_nat = sb("b_nat", [P, C, ER])
        b_twice = sb("b_twice", [P, C, 2, ER])
        bT_hi = sb("bT_hi", [P, D], f32r)
        bT_lo = sb("bT_lo", [P, D], f32r)
        w_sum = sb("w_sum", [P, D])
        ga_sum2 = sb("ga_sum2", [P, GA])
        ga_sum = sb("ga_sum", [P, GA])
        x_sb = sb("x_sb", [P, SLOTS, D])
        xb = sb("xb", [P, SLOTS, D])
        xb_part = sb("xb_part", [P, 2, D])
        y_hi = sb("y_hi", [P, 2, C, P], f32r)
        y_lo = sb("y_lo", [P, 2, C, P], f32r)
        ga_part = sb("ga_part", [P, GA])
        ga = sb("ga", [P, GA + 6])
        top8 = sb("top8", [P, 8])
        taken = sb("taken", [P, 8])
        rest = sb("rest", [P, E + 6])
        chosen = sb("chosen", [P, E])
        gap = sb("gap", [P, 2, E])
        gap_exp = sb("gap_exp", [P, 2, E])
        gate = sb("gate", [P, E])
        gate_total = sb("gate_total", [P, 1])
        gate_inv = sb("gate_inv", [P, 1])
        hs = sb("hs", [P, ER])
        hs_parts = sb("hs_parts", [P, 2, 2, ER])
        hsT = sb("hsT", [P, 2, P], f32r)
        o_sb = sb("o_sb", [P, SLOTS, D])

        ps = ctx.enter_context(nc.psum_tensor("ps", [P, 8, 512], f32))
        YT, GB, OB = 0, 2, 4
        HST_AT = 256

        ident_ready, zeros_ready, ones_ready = sem("ident_ready"), sem("zeros_ready"), sem("ones_ready")
        fill_step = sem("fill_step")
        cond_in, w0_in, w1_in, w2_in = sem("cond_in"), sem("w0_in"), sem("w1_in"), sem("w2_in")
        mix_in, w_in, ga_in, b_in = sem("mix_in"), sem("w_in"), sem("ga_in"), sem("b_in")
        condT_ps, condT_ready = sem("condT_ps"), sem("condT_ready")
        h_ps, h_ready = sem("h_ps"), sem("h_ready")
        logits_ps, att_step, att_exp_ready = sem("logits_ps"), sem("att_step"), sem("att_exp_ready")
        parts_ready, attT_ps, attT_ready = sem("parts_ready"), sem("attT_ps"), sem("attT_ready")
        mix_split = sem("mix_split")
        wT_ps, w_hi_ready, w_lo_ready = sem("wT_ps"), sem("w_hi_ready"), sem("w_lo_ready")
        gaT_ps, ga_hi_ready, ga_lo_ready = sem("gaT_ps"), sem("ga_hi_ready"), sem("ga_lo_ready")
        b_copied, bT_ps, b_hi_ready, b_lo_ready = sem("b_copied"), sem("bT_ps"), sem("b_hi_ready"), sem("b_lo_ready")
        agg_ps, agg_by_act, agg_by_dve, aggb_ready = sem("agg_ps"), sem("agg_by_act"), sem("agg_by_dve"), sem("aggb_ready")
        aggb_ps = sem("aggb_ps")
        wsum_ps, wsum_ready, gasum_ps, gasum_ready = sem("wsum_ps"), sem("wsum_ready"), sem("gasum_ps"), sem("gasum_ready")

        x_in = [sem(f"x_in{k}") for k in range(SLOTS)]
        stored = [sem(f"stored{k}") for k in range(SLOTS)]
        mixed = sem("mixed")
        yhi_ready, ylo_ready = sem("yhi_ready"), sem("ylo_ready")
        based = sem("based")
        gate_step = sem("gate_step")
        gap_ready, gap_exp_ready = sem("gap_ready"), sem("gap_exp_ready")
        hs_ready, hsT_ps, hsT_ready = sem("hs_ready"), sem("hsT_ps"), sem("hsT_ready")
        lora_done, out_ready = sem("lora_done"), sem("out_ready")
        xb_step, xb_ready = sem("xb_step"), sem("xb_ready")
        hs_step = sem("hs_step")
        LINKS = 9

        block = ctx.enter_context(nc.Block())

        @block.sync
        def _(sp):
            sp.dma_start(cond_sb[:], cond).then_inc(cond_in, 16)
            sp.dma_start(w0_sb[:], w0).then_inc(w0_in, 16)
            sp.dma_start(b0_col[:], b0.rearrange("(p a) -> p a", a=1)).then_inc(w0_in, 16)
            sp.dma_start(w_nat[:], w_base.rearrange("(a p) d -> p a d", p=P)).then_inc(w_in, 16)
            sp.dma_start(w1_sb[:], w1).then_inc(w1_in, 16)
            sp.dma_start(b1_col[:], b1.rearrange("(p a) -> p a", a=1)).then_inc(w1_in, 16)
            sp.dma_start(w2_sb[:], w2).then_inc(w2_in, 16)
            sp.dma_start(b2_row[:], b2.rearrange("(a k) -> a k", a=1)).then_inc(w2_in, 16)
            for k in range(SLOTS):
                sp.dma_start(x_sb[:, k], x_tiles[k]).then_inc(x_in[k], 16)

            def step(t, k, first, last, turn):
                if not first:
                    sp.wait_ge(out_ready, t)
                    sp.dma_start(out_tiles[t - 1], o_sb[:, (k - 1) % SLOTS]).then_inc(stored[(k - 1) % SLOTS], 16)
                if not turn:
                    sp.wait_ge(mixed, t + 1)
                    sp.wait_ge(xb_ready, t + 1)
                    sp.dma_start(x_sb[:, k], x_tiles[t + SLOTS]).then_inc(x_in[k], 16)

            for k in range(SLOTS):
                step(k, k, k == 0, False, False)
            with sp.Fori(1, GROUPS - 1) as g:
                for k in range(SLOTS):
                    step(g * SLOTS + k, k, False, False, False)
            for k in range(SLOTS):
                step((GROUPS - 1) * SLOTS + k, k, False, k == SLOTS - 1, True)
            sp.wait_ge(out_ready, TILES)
            sp.dma_start(out_tiles[TILES - 1], o_sb[:, SLOTS - 1]).then_inc(stored[SLOTS - 1], 16)
            for k in range(SLOTS):
                sp.wait_ge(stored[k], 16 * GROUPS)

        @block.gpsimd
        def _(pool):
            nc.gpsimd.memset(ident[:], 0.0).then_inc(fill_step, 1)
            nc.gpsimd.memset(mix_raw[:], 0.0).then_inc(zeros_ready, 1)
            pool.wait_ge(fill_step, 1)
            nc.gpsimd.affine_select(out=ident[:], in_=ident[:], compare_op=ALU.not_equal, fill=1.0, base=0,
                                    pattern=[[-1, P]], channel_multiplier=1).then_inc(ident_ready, 1)
            nc.gpsimd.memset(ones[:], 1.0).then_inc(ones_ready, 1)
            nc.gpsimd.memset(att_parts[:], 0.0).then_inc(ones_ready, 1)
            nc.gpsimd.memset(ones_r[:].bitcast(f32), 1.0).then_inc(ones_ready, 1)
            nc.gpsimd.memset(ga[:], LOW).then_inc(ones_ready, 1)
            nc.gpsimd.memset(taken[:], LOW).then_inc(ones_ready, 1)
            nc.gpsimd.memset(agg_bd[:], 0.0).then_inc(zeros_ready, 1)
            pool.wait_ge(mix_in, 16 * 8)
            nc.gpsimd.tensor_copy(mix_parts[:].bitcast(f32r), mix_raw[:]).then_inc(fill_step, 1)
            pool.wait_ge(fill_step, 2)
            half = slice(2 * QUAD, 4 * QUAD)
            nc.gpsimd.tensor_tensor(mix_parts[half], mix_raw[half], mix_parts[half], ALU.subtract).then_inc(fill_step, 1)
            pool.wait_ge(fill_step, 3)
            for s in range(SPT):
                nc.gpsimd.tensor_copy(mix_reps[:, :, s], mix_parts[:]).then_inc(mix_split, 1)
            pool.wait_ge(b_in, 16 * C)
            nc.gpsimd.tensor_copy(b_twice[:, :, 0], b_nat[:]).then_inc(b_copied, 1)
            nc.gpsimd.tensor_copy(b_twice[:, :, 1], b_nat[:]).then_inc(b_copied, 1)
            pool.wait_ge(wsum_ready, 1)
            pool.wait_ge(aggb_ready, SPT)

            def step(t, k, turn, peeled):
                pool.wait_ge(x_in[k], 16 * turn + 16)
                nc.gpsimd.tensor_tensor(xb_part[:, k % 2], w_sum[:],
                                        agg_b[:, bass.ds(t, 1)].to_broadcast([P, D]), ALU.mult).then_inc(xb_step, 1)
                pool.wait_ge(xb_step, t + 1)
                if not peeled:
                    pool.wait_ge(out_ready, t - SLOTS + 1)
                nc.gpsimd.tensor_tensor(xb[:, k], xb_part[:, k % 2], x_sb[:, k], ALU.add).then_inc(xb_ready, 1)

            for k in range(SLOTS):
                step(k, k, 0, True)
            with pool.Fori(1, GROUPS) as g:
                for k in range(SLOTS):
                    step(g * SLOTS + k, k, g, False)

        def copy_agg(copy, r, done):
            bank = 4 + 2 * (r % 2)
            for s in range(SPT):
                rows = slice(s * CH, (s + 1) * CH)
                src = ps[rows, bank:bank + 2, :].rearrange("p a n -> p (a n)") \
                    .rearrange("p (o t s) -> p s t o", s=SPT, t=TILES)[:, s]
                dst = agg_bd[rows, :, s, r * PER_ROUND:(r + 1) * PER_ROUND]
                copy(dst, src).then_inc(done, 1)

        @block.scalar
        def _(act):
            act.dma_start(ga_nat[0:ER, :], lora_a.rearrange("e r d -> (e r) d")).then_inc(ga_in, 16)
            act.dma_start(ga_nat[ER:GA, :], gate_w).then_inc(ga_in, 16)
            act.wait_ge(zeros_ready, 1)
            for q in range(4):
                rows = slice(q * QUAD, q * QUAD + K)
                act.dma_start(mix_raw[rows, 0:CH, :], mix_w.rearrange("k o i a -> k o (i a)")).then_inc(mix_in, 16)
                act.dma_start(mix_raw[rows, CH, :], mix_b).then_inc(mix_in, 16)
            for a in range(C):
                act.dma_start(b_nat[:, a].rearrange("p (e r) -> p e r", e=E),
                              lora_b.rearrange("e (a p) r -> a p e r", p=P)[a]).then_inc(b_in, 16)

            def w_hi(c):
                act.wait_ge(wT_ps, c + 1)
                nc.scalar.activation(wT_hi[:, c, :], ps[:, 4 + c, :], ACT.Copy).then_inc(w_hi_ready, 1)

            act.wait_ge(h_ps, 1)
            nc.scalar.activation(h1T[:], ps[:, 1, 0:P], ACT.Gelu, bias=b0_col[:]).then_inc(h_ready, 1)
            w_hi(0)
            act.wait_ge(h_ps, 2)
            act.wait_ge(w1_in, 32)
            nc.scalar.activation(h2T[:], ps[:, 2, 0:P], ACT.Gelu, bias=b1_col[:]).then_inc(h_ready, 1)
            w_hi(1)
            act.wait_ge(att_step, 2)
            nc.scalar.activation(att_exp[:], ps[:, 3, 0:K], ACT.Exp, bias=att_neg[:],
                                 accum_out=att_sum[:]).then_inc(att_exp_ready, 1)
            w_hi(2)
            w_hi(3)
            act.wait_ge(gaT_ps, 1)
            nc.scalar.activation(gaT[:, :, 0, :], ps[:, 0, 0:C * GA].rearrange("p (c n) -> p c n", c=C),
                                 ACT.Copy).then_inc(ga_hi_ready, 1)
            act.wait_ge(zeros_ready, 2)
            for r in range(1, ROUNDS, 2):
                act.wait_ge(agg_ps, r + 1)
                copy_agg(nc.scalar.copy, r, agg_by_act)
            act.wait_ge(bT_ps, 1)
            nc.scalar.activation(bT_hi[:], ps[:, 2, :], ACT.Copy).then_inc(b_hi_ready, 1)
            act.wait_ge(wsum_ps, 1)
            nc.scalar.activation(w_sum[:], ps[:, 3, :], ACT.Copy).then_inc(wsum_ready, 1)
            act.wait_ge(gasum_ps, 1)
            nc.scalar.activation(ga_sum2[:], ps[:, 1, GA:2 * GA], ACT.Copy).then_inc(gasum_ready, 1)

            def yhi(t, k):
                act.wait_ge(mixed, t + 1)
                if not (isinstance(t, int) and t < 2):
                    act.wait_ge(based, t - 1)
                nc.scalar.activation(y_hi[:, k % 2], ps[:, YT + k % 2, :].rearrange("p (c n) -> p c n", c=C),
                                     ACT.Copy).then_inc(yhi_ready, 1)

            def exp_gap(t, k):
                act.wait_ge(gap_ready, t + 1)
                nc.scalar.activation(gap_exp[:, k % 2], gap[:, k % 2], ACT.Exp).then_inc(gap_exp_ready, 1)

            def copy_hsT(t, k):
                act.wait_ge(hsT_ps, t + 1)
                nc.scalar.activation(hsT[:, k % 2], ps[:, GB + k % 2, HST_AT:HST_AT + P], ACT.Copy,
                                     scale=2.0).then_inc(hsT_ready, 1)

            yhi(0, 0)

            def step(t, k, first, last):
                if not first:
                    exp_gap(t - 1, (k - 1) % SLOTS)
                if not last:
                    yhi(t + 1, k + 1)
                if not first:
                    copy_hsT(t - 1, (k - 1) % SLOTS)

            for k in range(SLOTS):
                step(k, k, k == 0, False)
            with act.Fori(1, GROUPS - 1) as g:
                for k in range(SLOTS):
                    step(g * SLOTS + k, k, False, False)
            for k in range(SLOTS):
                step((GROUPS - 1) * SLOTS + k, k, False, k == SLOTS - 1)
            exp_gap(TILES - 1, SLOTS - 1)
            copy_hsT(TILES - 1, SLOTS - 1)

        @block.vector
        def _(dve):
            dve.wait_ge(condT_ps, 1)
            nc.vector.tensor_copy(condT[:], ps[:, 0, 0:P]).then_inc(condT_ready, 1)

            def w_lo(c):
                dve.wait_ge(w_hi_ready, c + 1)
                nc.vector.tensor_tensor(wT_lo[:, c, :], ps[:, 4 + c, :], wT_hi[:, c, :].bitcast(f32),
                                        ALU.subtract).then_inc(w_lo_ready, 1)

            w_lo(0)
            w_lo(1)
            dve.wait_ge(logits_ps, 1)
            nc.vector.reduce_max(att_max[:], ps[:, 3, 0:K], AX.X).then_inc(att_step, 1)
            dve.wait_ge(att_step, 1)
            nc.vector.tensor_scalar(att_neg[:], att_max[:], -1.0, None, ALU.mult).then_inc(att_step, 1)
            dve.wait_ge(att_exp_ready, 1)
            nc.vector.reciprocal(att_inv[:], att_sum[:]).then_inc(att_step, 1)
            dve.wait_ge(att_step, 3)
            nc.vector.tensor_scalar(att[:], att_exp[:], att_inv[:], None, ALU.mult).then_inc(att_step, 1)
            dve.wait_ge(att_step, 4)
            dve.wait_ge(ones_ready, 5)
            pairs = att_parts[:].rearrange("p (a n) -> p a n", a=2)
            twice = att[:].rearrange("p (a n) -> p a n", a=1).to_broadcast([P, 2, K])
            nc.vector.tensor_copy(pairs[:, :, 0:K].bitcast(f32r), twice).then_inc(att_step, 1)
            dve.wait_ge(att_step, 5)
            nc.vector.tensor_tensor(pairs[:, :, QUAD:QUAD + K], twice, pairs[:, :, 0:K],
                                    ALU.subtract).then_inc(parts_ready, 1)
            dve.wait_ge(attT_ps, 1)
            nc.vector.tensor_copy(attT[:], ps[:, 1, 0:BATCH]).then_inc(attT_ready, 1)
            w_lo(2)
            w_lo(3)
            dve.wait_ge(ga_hi_ready, 1)
            nc.vector.tensor_tensor(gaT[:, :, 1, :], ps[:, 0, 0:C * GA].rearrange("p (c n) -> p c n", c=C),
                                    gaT[:, :, 0, :].bitcast(f32), ALU.subtract).then_inc(ga_lo_ready, 1)
            dve.wait_ge(aggb_ps, 1)
            for s in range(SPT):
                rows = slice(s * CH, (s + 1) * CH)
                nc.vector.tensor_copy(agg_b[rows, :], ps[rows, 1, 256:256 + BATCH]
                                      .rearrange("p (t s) -> p s t", s=SPT)[:, s]).then_inc(aggb_ready, 1)
            dve.wait_ge(zeros_ready, 2)
            for r in range(0, ROUNDS, 2):
                dve.wait_ge(agg_ps, r + 1)
                copy_agg(nc.vector.tensor_copy, r, agg_by_dve)
            dve.wait_ge(b_hi_ready, 1)
            nc.vector.tensor_tensor(bT_lo[:], ps[:, 2, :], bT_hi[:].bitcast(f32), ALU.subtract).then_inc(b_lo_ready, 1)
            dve.wait_ge(gasum_ready, 1)
            nc.vector.tensor_tensor(ga_sum[:], ps[:, 1, 0:GA], ga_sum2[:], ALU.add).then_inc(gasum_ready, 1)
            dve.wait_ge(gasum_ready, 2)
            dve.wait_ge(aggb_ready, SPT)

            def ylo(t, k):
                dve.wait_ge(yhi_ready, t + 1)
                nc.vector.tensor_tensor(y_lo[:, k % 2], ps[:, YT + k % 2, :].rearrange("p (c n) -> p c n", c=C),
                                        y_hi[:, k % 2].bitcast(f32), ALU.subtract).then_inc(ylo_ready, 1)

            def gating(t, k):
                at = LINKS * t
                bank = GB + k % 2
                gp = k % 2

                def link(ins, n):
                    ins.then_inc(gate_step, 1)
                    dve.wait_ge(gate_step, at + n)

                dve.wait_ge(based, t + 1)
                link(nc.vector.scalar_tensor_tensor(out=ga_part[:], in0=ga_sum[:], scalar=agg_b[:, bass.ds(t, 1)],
                                                    in1=ps[:, bank, GA:2 * GA], op0=ALU.mult, op1=ALU.add), 1)
                link(nc.vector.tensor_tensor(ga[:, ER:GA], ps[:, bank, ER:GA], ga_part[:, ER:GA], ALU.add), 2)
                nc.vector.tensor_tensor(ga[:, 0:ER], ps[:, bank, 0:ER], ga_part[:, 0:ER], ALU.add).then_inc(gate_step, 1)
                nc.vector.max(top8[:], ga[:, ER:GA]).then_inc(gate_step, 1)
                dve.wait_ge(gate_step, at + 4)
                link(nc.vector.tensor_copy(taken[:, 0:2], top8[:, 0:2]), 5)
                nc.vector.tensor_scalar(gap[:, gp], ga[:, ER:GA], top8[:, 0:1], None, ALU.subtract).then_inc(gap_ready, 1)
                link(nc.vector.match_replace(rest[:], taken[:], ga[:, ER:GA + 6], LOW), 6)
                nc.vector.tensor_tensor(chosen[:], rest[:, 0:E], ga[:, ER:GA], ALU.not_equal).then_inc(gate_step, 1)
                dve.wait_ge(gate_step, at + 7)
                dve.wait_ge(gap_exp_ready, t + 1)
                nc.vector.scalar_tensor_tensor(out=gate[:], in0=gap_exp[:, gp], scalar=1.0, in1=chosen[:],
                                               op0=ALU.mult, op1=ALU.mult,
                                               accum_out=gate_total[:]).then_inc(gate_step, 1)
                dve.wait_ge(gate_step, at + 8)
                nc.vector.reciprocal(gate_inv[:], gate_total[:]).then_inc(gate_step, 1)
                dve.wait_ge(gate_step, at + 9)
                nc.vector.scalar_tensor_tensor(
                    out=hs[:].rearrange("p (e r) -> p e r", e=E), in0=ga[:, 0:ER].rearrange("p (e r) -> p e r", e=E),
                    scalar=gate_inv[:], in1=gate[:].rearrange("p (e a) -> p e a", a=1).to_broadcast([P, E, R]),
                    op0=ALU.mult, op1=ALU.mult).then_inc(hs_step, 1)
                dve.wait_ge(hs_step, 2 * t + 1)
                nc.vector.tensor_copy(hs_parts[:, gp, 0].bitcast(f32r), hs[:]).then_inc(hs_step, 1)
                dve.wait_ge(hs_step, 2 * t + 2)
                nc.vector.tensor_tensor(hs_parts[:, gp, 1], hs[:], hs_parts[:, gp, 0], ALU.subtract).then_inc(hs_ready, 1)

            def finish(t, k, turn, peeled):
                dve.wait_ge(lora_done, t + 1)
                dve.wait_ge(xb_ready, t + 1)
                if not peeled:
                    dve.wait_ge(stored[k], 16 * turn)
                nc.vector.tensor_tensor(o_sb[:, k], ps[:, OB + k, :], xb[:, k], ALU.add).then_inc(out_ready, 1)

            ylo(0, 0)

            def step(t, k, turn, first, last, peeled):
                if not first:
                    gating(t - 1, (k - 1) % SLOTS)
                if not last:
                    ylo(t + 1, k + 1)
                if not first:
                    back = 1 if k == 0 else 0
                    finish(t - 1, (k - 1) % SLOTS, turn - back, peeled)

            for k in range(SLOTS):
                step(k, k, 0, k == 0, False, True)
            step(SLOTS, 0, 1, False, False, True)
            for k in range(1, SLOTS):
                step(SLOTS + k, k, 1, False, False, False)
            with dve.Fori(2, GROUPS - 1) as g:
                for k in range(SLOTS):
                    step(g * SLOTS + k, k, g, False, False, False)
            for k in range(SLOTS):
                step((GROUPS - 1) * SLOTS + k, k, GROUPS - 1, False, k == SLOTS - 1, False)
            gating(TILES - 1, SLOTS - 1)
            finish(TILES - 1, SLOTS - 1, GROUPS - 1, False)



        @block.tensor
        def _(pe):
            def transposes_of_w(c):
                for a in range(C):
                    last = nc.tensor.transpose(ps[:, 4 + c, a * P:(a + 1) * P], w_nat[:, a, c * P:(c + 1) * P], ident[:])
                last.then_inc(wT_ps, 1)

            pe.wait_ge(ident_ready, 1)
            pe.wait_ge(cond_in, 16)
            nc.tensor.transpose(ps[:, 0, 0:P], cond_sb[:], ident[:]).then_inc(condT_ps, 1)
            pe.wait_ge(condT_ready, 1)
            pe.wait_ge(w0_in, 32)
            nc.tensor.matmul(ps[:, 1, 0:P], w0_sb[:], condT[:], start=True, stop=True).then_inc(h_ps, 1)
            pe.wait_ge(w_in, 16)
            transposes_of_w(0)
            pe.wait_ge(h_ready, 1)
            pe.wait_ge(w1_in, 32)
            nc.tensor.matmul(ps[:, 2, 0:P], w1_sb[:], h1T[:], start=True, stop=True).then_inc(h_ps, 1)
            transposes_of_w(1)
            pe.wait_ge(h_ready, 2)
            pe.wait_ge(w2_in, 32)
            pe.wait_ge(ones_ready, 5)
            nc.tensor.matmul(ps[:, 3, 0:K], h2T[:], w2_sb[:], start=True, stop=False)
            nc.tensor.matmul(ps[:, 3, 0:K], ones[0:1, :], b2_row[:], start=False, stop=True).then_inc(logits_ps, 1)
            transposes_of_w(2)
            transposes_of_w(3)
            pe.wait_ge(ga_in, 32)
            for c in range(C):
                last = nc.tensor.transpose(ps[:, 0, c * GA:(c + 1) * GA], ga_nat[:, c * P:(c + 1) * P],
                                           ident[0:GA, 0:GA])
            last.then_inc(gaT_ps, 1)
            pe.wait_ge(parts_ready, 1)
            nc.tensor.transpose(ps[:, 1, 0:BATCH], att_parts[:], ident[:]).then_inc(attT_ps, 1)
            pe.wait_ge(attT_ready, 1)
            pe.wait_ge(mix_split, SPT)

            def kernels(o):
                return mix_reps[:, o].rearrange("p s i -> p (s i)")

            nc.tensor.matmul(ps[:, 1, 256:256 + BATCH], kernels(CH), attT[:], start=True, stop=True).then_inc(aggb_ps, 1)
            for r in range(ROUNDS):
                bank = 4 + 2 * (r % 2)
                if r < 2:
                    pe.wait_ge(w_lo_ready, 2 * r + 2)
                else:
                    pe.wait_ge(agg_by_dve if r % 2 == 0 else agg_by_act, SPT * (r // 2))
                for n in range(PER_ROUND):
                    at = (n % (PER_ROUND // 2)) * BATCH
                    last = nc.tensor.matmul(ps[:, bank + n // (PER_ROUND // 2), at:at + BATCH],
                                            kernels(r * PER_ROUND + n), attT[:], start=True, stop=True)
                last.then_inc(agg_ps, 1)
            pe.wait_ge(b_copied, 2)
            for a in range(C):
                last = nc.tensor.transpose(ps[:, 2, a * P:(a + 1) * P], b_twice[:, a].rearrange("p h n -> p (h n)"), ident[:])
            last.then_inc(bT_ps, 1)
            pe.wait_ge(w_lo_ready, C)
            for c in range(C):
                nc.tensor.matmul(ps[:, 3, :], ones_r[:], wT_hi[:, c, :], start=(c == 0), stop=False)
                last = nc.tensor.matmul(ps[:, 3, :], ones_r[:], wT_lo[:, c, :], start=False, stop=(c == C - 1))
            last.then_inc(wsum_ps, 1)
            pe.wait_ge(ga_lo_ready, 1)
            pe.wait_ge(aggb_ready, SPT)
            for c in range(C):
                last = nc.tensor.matmul(ps[:, 1, 0:2 * GA], ones_r[:], gaT[:, c].rearrange("p h n -> p (h n)"),
                                        start=(c == 0), stop=(c == C - 1))
            last.then_inc(gasum_ps, 1)

            def mix(t, k, turn):
                pe.wait_ge(x_in[k], 16 * turn + 16)
                rhs = agg_bd[:].rearrange("p t s o -> p t (s o)")[:, bass.ds(t, 1), :].rearrange("p t n -> p (t n)")
                for c in range(C):
                    last = nc.tensor.matmul(ps[:, YT + k % 2, c * P:(c + 1) * P], x_sb[:, k, c * P:(c + 1) * P],
                                            rhs, start=True, stop=True)
                last.then_inc(mixed, 1)

            def base_chunk(t, k, c):
                o, g = ps[:, OB + k, :], ps[:, GB + k % 2, :]
                hi, lo = y_hi[:, k % 2, c], y_lo[:, k % 2, c]
                both = gaT[:, c].rearrange("p h n -> p (h n)")
                if c == 0:
                    pe.wait_ge(yhi_ready, t + 1)
                nc.tensor.matmul(o, hi, wT_hi[:, c, :], start=(c == 0), stop=False)
                nc.tensor.matmul(o, hi, wT_lo[:, c, :], start=False, stop=False)
                nc.tensor.matmul(g[:, 0:2 * GA], hi, both, start=(c == 0), stop=False)
                if c == 0:
                    pe.wait_ge(ylo_ready, t + 1)
                nc.tensor.matmul(o, lo, wT_hi[:, c, :], start=False, stop=False)
                return nc.tensor.matmul(g[:, 0:2 * GA], lo, both, start=False, stop=(c == C - 1))

            def turn_hs(t, k):
                pe.wait_ge(hs_ready, t + 1)
                nc.tensor.transpose(ps[:, GB + k % 2, HST_AT:HST_AT + P],
                                    hs_parts[:, k % 2].rearrange("p h n -> p (h n)"), ident[:]).then_inc(hsT_ps, 1)

            def lora(t, k):
                pe.wait_ge(hsT_ready, t + 1)
                nc.tensor.matmul(ps[:, OB + k, :], hsT[:, k % 2], bT_hi[:], start=False, stop=False)
                nc.tensor.matmul(ps[:, OB + k, :], hsT[:, k % 2], bT_lo[:], start=False, stop=True).then_inc(lora_done, 1)

            def step(t, k, turn, first, last, peeled):
                if not last:
                    mix(t + 1, (k + 1) % SLOTS, turn + (1 if k == SLOTS - 1 else 0))
                if not peeled:
                    pe.wait_ge(out_ready, t - SLOTS + 1)
                for c in range(C - 1):
                    base_chunk(t, k, c)
                if not first:
                    turn_hs(t - 1, (k - 1) % SLOTS)
                base_chunk(t, k, C - 1).then_inc(based, 1)
                if not first:
                    lora(t - 1, (k - 1) % SLOTS)

            pe.wait_ge(agg_by_dve, SPT * (ROUNDS // 2))
            pe.wait_ge(agg_by_act, SPT * (ROUNDS // 2))
            pe.wait_ge(ga_lo_ready, 1)
            mix(0, 0, 0)
            pe.wait_ge(gasum_ready, 2)
            pe.wait_ge(wsum_ready, 1)
            pe.wait_ge(b_lo_ready, 1)
            for k in range(SLOTS):
                step(k, k, 0, k == 0, False, True)
            with pe.Fori(1, GROUPS - 1) as g:
                for k in range(SLOTS):
                    step(g * SLOTS + k, k, g, False, False, False)
            for k in range(SLOTS):
                step((GROUPS - 1) * SLOTS + k, k, GROUPS - 1, False, k == SLOTS - 1, False)
            turn_hs(TILES - 1, SLOTS - 1)
            lora(TILES - 1, SLOTS - 1)


_INS = ["x", "cond_128", "L0_cond_W0", "L0_cond_b0", "L0_cond_W1", "L0_cond_b1", "L0_cond_W2", "L0_cond_b2",
        "L0_cond_weight", "L0_cond_bias_k", "L0_ffn_W_base", "L0_ffn_gate_W", "L0_ffn_A", "L0_ffn_B"]


def kernel(**inputs):
    import numpy as _np
    import concourse.bacc as _bacc
    from concourse import mybir as _mybir
    from concourse.bass_utils import run_bass_kernel_spmd as _run

    nc = _bacc.Bacc("TRN2", target_bir_lowering=False, num_devices=1)
    arrays, args = {}, []
    for name in _INS:
        a = _np.ascontiguousarray(inputs[name])
        arrays[f"in_{name}_dram"] = a
        args.append(nc.dram_tensor(f"in_{name}_dram", a.shape, _mybir.dt.from_np(a.dtype), kind="ExternalInput").ap())
    args.append(nc.dram_tensor("out_dram", inputs["x"].shape, _mybir.dt.float32, kind="ExternalOutput").ap())
    adaln_moe_ffn_kernel(nc, *args)
    r = _run(nc, [arrays], core_ids=[0])
    return r.results[0]["out_dram"]
```

```python
import concourse.bass as bass
from concourse import mybir
from contextlib import ExitStack


def adaln_moe_ffn_kernel(nc, x, cond, w0, b0, w1, b1, w2, b2, mix_w, mix_b, w_base, gate_w, lora_a, lora_b, out):
    f32, f32r = mybir.dt.float32, mybir.dt.float32r
    ALU = mybir.AluOpType
    ACT = mybir.ActivationFunctionType
    AX = mybir.AxisListType

    P = 128
    BATCH, CH, D = x.shape
    K = mix_w.shape[0]
    E, R, _ = lora_a.shape
    ER = E * R
    GA = ER + E
    SPT = P // CH
    TILES = BATCH // SPT
    C = D // P
    SLOTS = 4
    GROUPS = TILES // SLOTS
    HALF = D // 2
    WIDE = D + GA
    LOW = -3.0e38
    PER_ROUND = 8
    ROUNDS = CH // PER_ROUND

    x_tiles = x.rearrange("(t s) c d -> t (s c) d", s=SPT)
    out_tiles = out.rearrange("(t s) c d -> t (s c) d", s=SPT)

    ctx = ExitStack()
    with ctx:
        def sb(name, shape, dt=f32):
            return ctx.enter_context(nc.sbuf_tensor(name, shape, dt))

        def sem(name):
            return ctx.enter_context(nc.semaphore(name))

        ident = sb("ident", [P, P])
        ones = sb("ones", [P, P])
        ones_r = sb("ones_r", [P, P], f32r)
        cond_sb = sb("cond_sb", [P, P])
        condT = sb("condT", [P, P])
        w0_sb = sb("w0_sb", [P, P])
        w1_sb = sb("w1_sb", [P, P])
        w2_sb = sb("w2_sb", [P, K])
        b0_col = sb("b0_col", [P, 1])
        b1_col = sb("b1_col", [P, 1])
        b2_row = sb("b2_row", [1, K])
        h1T = sb("h1T", [P, P])
        h2T = sb("h2T", [P, P])
        att_max = sb("att_max", [P, 1])
        att_neg = sb("att_neg", [P, 1])
        att_exp = sb("att_exp", [P, K])
        att_sum = sb("att_sum", [P, 1])
        att_inv = sb("att_inv", [P, 1])
        att = sb("att", [P, K])
        attT = sb("attT", [K, BATCH])
        mix_reps = sb("mix_reps", [K, CH + 1, SPT, CH])
        agg_bd = sb("agg_bd", [P, TILES, SPT, CH])
        agg_b = sb("agg_b", [P, TILES])
        w_nat = sb("w_nat", [P, C, D])
        wT_hi = sb("wT_hi", [P, C, WIDE], f32r)
        wT_lo = sb("wT_lo", [P, C, WIDE], f32r)
        ga_nat = sb("ga_nat", [GA, D])
        b_nat = sb("b_nat", [P, C, ER])
        b_twice = sb("b_twice", [P, C, 2, ER])
        bT_hi = sb("bT_hi", [P, D], f32r)
        bT_lo = sb("bT_lo", [P, D], f32r)
        w_sum = sb("w_sum", [P, D])
        ga_sum = sb("ga_sum", [P, GA])
        x_sb = sb("x_sb", [P, SLOTS, D])
        xb = sb("xb", [P, SLOTS, D])
        xb_part = sb("xb_part", [P, 2, D])
        y_hi = sb("y_hi", [P, 2, C, P], f32r)
        y_lo = sb("y_lo", [P, 2, C, P], f32r)
        ga = sb("ga", [P, GA + 6])
        top8 = sb("top8", [P, 8])
        taken = sb("taken", [P, 8])
        rest = sb("rest", [P, E + 6])
        chosen = sb("chosen", [P, E])
        gap = sb("gap", [P, 2, E])
        gap_exp = sb("gap_exp", [P, 2, E])
        gate = sb("gate", [P, E])
        gate_total = sb("gate_total", [P, 1])
        gate_inv = sb("gate_inv", [P, 1])
        hs = sb("hs", [P, ER])
        hs_parts = sb("hs_parts", [P, 2, 2, ER])
        hsT = sb("hsT", [P, 2, P], f32r)
        o_sb = sb("o_sb", [P, SLOTS, D])

        ps = ctx.enter_context(nc.psum_tensor("ps", [P, 8, 512], f32))
        YT, HT, OA, OB = 0, 2, 4, 6

        ident_ready, zeros_ready, ones_ready = sem("ident_ready"), sem("zeros_ready"), sem("ones_ready")
        fill_step = sem("fill_step")
        cond_in, w0_in, w1_in, w2_in = sem("cond_in"), sem("w0_in"), sem("w1_in"), sem("w2_in")
        mixb_in = sem("mixb_in")
        mix_in, w_in, ga_in, b_in = sem("mix_in"), sem("w_in"), sem("ga_in"), sem("b_in")
        condT_ps, condT_ready = sem("condT_ps"), sem("condT_ready")
        h_ps, h_ready = sem("h_ps"), sem("h_ready")
        logits_ps, att_step, att_exp_ready = sem("logits_ps"), sem("att_step"), sem("att_exp_ready")
        att_ready, attT_ps, attT_ready = sem("att_ready"), sem("attT_ps"), sem("attT_ready")
        wT_ps, w_hi_ready, w_lo_ready = sem("wT_ps"), sem("w_hi_ready"), sem("w_lo_ready")
        gaT_ps, ga_hi_ready, ga_lo_ready = sem("gaT_ps"), sem("ga_hi_ready"), sem("ga_lo_ready")
        b_copied, bT_ps, b_hi_ready, b_lo_ready = sem("b_copied"), sem("bT_ps"), sem("b_hi_ready"), sem("b_lo_ready")
        agg_ps, agg_by_act, agg_by_dve, aggb_ready = sem("agg_ps"), sem("agg_by_act"), sem("agg_by_dve"), sem("aggb_ready")
        aggb_ps = sem("aggb_ps")
        wsum_ps, wsum_ready, gasum_ps, gasum_ready = sem("wsum_ps"), sem("wsum_ready"), sem("gasum_ps"), sem("gasum_ready")

        x_in = [sem(f"x_in{k}") for k in range(SLOTS)]
        stored = [sem(f"stored{k}") for k in range(SLOTS)]
        mixed = sem("mixed")
        yhi_ready, ylo_ready = sem("yhi_ready"), sem("ylo_ready")
        ga_done = sem("ga_done")
        gate_step = sem("gate_step")
        gap_ready, gap_exp_ready = sem("gap_ready"), sem("gap_exp_ready")
        hs_ready, hsT_ps, hsT_ready = sem("hs_ready"), sem("hsT_ps"), sem("hsT_ready")
        lora_done, half_ready, out_ready = sem("lora_done"), sem("half_ready"), sem("out_ready")
        xb_step, xb_ready = sem("xb_step"), sem("xb_ready")
        hs_step = sem("hs_step")
        LINKS = 8

        block = ctx.enter_context(nc.Block())

        @block.sync
        def _(sp):
            sp.dma_start(cond_sb[:], cond).then_inc(cond_in, 16)
            sp.dma_start(b0_col[:], b0.rearrange("(p a) -> p a", a=1)).then_inc(w0_in, 16)
            sp.dma_start(w1_sb[:], w1).then_inc(w1_in, 16)
            sp.dma_start(w2_sb[:], w2).then_inc(w2_in, 16)
            for s in range(SPT):
                sp.dma_start(mix_reps[:, 0:CH, s, :], mix_w.rearrange("k o i a -> k o (i a)")).then_inc(mix_in, 16)
            for k in range(SLOTS):
                sp.dma_start(x_sb[:, k], x_tiles[k]).then_inc(x_in[k], 16)

            def step(t, k, first, last, turn):
                if not first:
                    sp.wait_ge(out_ready, t)
                    sp.dma_start(out_tiles[t - 1], o_sb[:, (k - 1) % SLOTS]).then_inc(stored[(k - 1) % SLOTS], 16)
                if not turn:
                    sp.wait_ge(mixed, t + 1)
                    sp.wait_ge(xb_ready, t + 1)
                    sp.dma_start(x_sb[:, k], x_tiles[t + SLOTS]).then_inc(x_in[k], 16)

            for k in range(SLOTS):
                step(k, k, k == 0, False, False)
            with sp.Fori(1, GROUPS - 1) as g:
                for k in range(SLOTS):
                    step(g * SLOTS + k, k, False, False, False)
            for k in range(SLOTS):
                step((GROUPS - 1) * SLOTS + k, k, False, k == SLOTS - 1, True)
            sp.wait_ge(out_ready, TILES)
            sp.dma_start(out_tiles[TILES - 1], o_sb[:, SLOTS - 1]).then_inc(stored[SLOTS - 1], 16)
            for k in range(SLOTS):
                sp.wait_ge(stored[k], 16 * GROUPS)

        @block.gpsimd
        def _(pool):
            nc.gpsimd.memset(ident[:], 0.0).then_inc(fill_step, 1)
            pool.wait_ge(fill_step, 1)
            nc.gpsimd.affine_select(out=ident[:], in_=ident[:], compare_op=ALU.not_equal, fill=1.0, base=0,
                                    pattern=[[-1, P]], channel_multiplier=1).then_inc(ident_ready, 1)
            pool.dma_start(ga_nat[0:ER, :], lora_a.rearrange("e r d -> (e r) d")).then_inc(ga_in, 16)
            pool.dma_start(ga_nat[ER:GA, :], gate_w).then_inc(ga_in, 16)
            for s in range(SPT):
                pool.dma_start(mix_reps[:, CH, s, :], mix_b).then_inc(mixb_in, 16)
            for a in range(C):
                pool.dma_start(b_nat[:, a].rearrange("p (e r) -> p e r", e=E),
                               lora_b.rearrange("e (a p) r -> a p e r", p=P)[a]).then_inc(b_in, 16)
            nc.gpsimd.memset(ones[:], 1.0).then_inc(ones_ready, 1)
            nc.gpsimd.memset(ones_r[:].bitcast(f32), 1.0).then_inc(ones_ready, 1)
            nc.gpsimd.memset(ga[:], LOW).then_inc(ones_ready, 1)
            nc.gpsimd.memset(taken[:], LOW).then_inc(ones_ready, 1)
            nc.gpsimd.memset(agg_bd[:], 0.0).then_inc(zeros_ready, 1)
            pool.wait_ge(b_in, 16 * C)
            nc.gpsimd.tensor_copy(b_twice[:, :, 0], b_nat[:]).then_inc(b_copied, 1)
            nc.gpsimd.tensor_copy(b_twice[:, :, 1], b_nat[:]).then_inc(b_copied, 1)
            pool.wait_ge(wsum_ready, 1)
            pool.wait_ge(aggb_ready, SPT)

            def step(t, k, turn, peeled):
                pool.wait_ge(x_in[k], 16 * turn + 16)
                nc.gpsimd.tensor_tensor(xb_part[:, k % 2], w_sum[:],
                                        agg_b[:, bass.ds(t, 1)].to_broadcast([P, D]), ALU.mult).then_inc(xb_step, 1)
                pool.wait_ge(xb_step, t + 1)
                if not peeled:
                    pool.wait_ge(out_ready, t - SLOTS + 1)
                nc.gpsimd.tensor_tensor(xb[:, k], xb_part[:, k % 2], x_sb[:, k], ALU.add).then_inc(xb_ready, 1)

            for k in range(SLOTS):
                step(k, k, 0, True)
            with pool.Fori(1, GROUPS) as g:
                for k in range(SLOTS):
                    step(g * SLOTS + k, k, g, False)

        def copy_agg(copy, r, done):
            bank = 4 + 2 * (r % 2)
            for s in range(SPT):
                rows = slice(s * CH, (s + 1) * CH)
                src = ps[rows, bank:bank + 2, :].rearrange("p a n -> p (a n)") \
                    .rearrange("p (o t s) -> p s t o", s=SPT, t=TILES)[:, s]
                dst = agg_bd[rows, :, s, r * PER_ROUND:(r + 1) * PER_ROUND]
                copy(dst, src).then_inc(done, 1)

        @block.scalar
        def _(act):
            act.dma_start(w0_sb[:], w0).then_inc(w0_in, 16)
            act.dma_start(b1_col[:], b1.rearrange("(p a) -> p a", a=1)).then_inc(w1_in, 16)
            act.dma_start(b2_row[:], b2.rearrange("(a k) -> a k", a=1)).then_inc(w2_in, 16)
            act.dma_start(w_nat[:], w_base.rearrange("(a p) d -> p a d", p=P)).then_inc(w_in, 16)

            def w_hi(c):
                act.wait_ge(wT_ps, c + 1)
                nc.scalar.activation(wT_hi[:, c, 0:D], ps[:, 4 + c, :], ACT.Copy).then_inc(w_hi_ready, 1)

            act.wait_ge(h_ps, 1)
            nc.scalar.activation(h1T[:], ps[:, 1, 0:P], ACT.Gelu, bias=b0_col[:]).then_inc(h_ready, 1)
            w_hi(0)
            act.wait_ge(h_ps, 2)
            act.wait_ge(w1_in, 32)
            nc.scalar.activation(h2T[:], ps[:, 2, 0:P], ACT.Gelu, bias=b1_col[:]).then_inc(h_ready, 1)
            w_hi(1)
            act.wait_ge(att_step, 2)
            nc.scalar.activation(att_exp[:], ps[:, 3, 0:K], ACT.Exp, bias=att_neg[:],
                                 accum_out=att_sum[:]).then_inc(att_exp_ready, 1)
            w_hi(2)
            w_hi(3)
            act.wait_ge(gaT_ps, 1)
            nc.scalar.activation(wT_hi[:, :, D:WIDE], ps[:, 0, 0:C * GA].rearrange("p (c n) -> p c n", c=C),
                                 ACT.Copy).then_inc(ga_hi_ready, 1)
            act.wait_ge(zeros_ready, 1)
            for r in range(1, ROUNDS, 2):
                act.wait_ge(agg_ps, r + 1)
                copy_agg(nc.scalar.copy, r, agg_by_act)
            act.wait_ge(bT_ps, 1)
            nc.scalar.activation(bT_hi[:], ps[:, 2, :], ACT.Copy).then_inc(b_hi_ready, 1)
            act.wait_ge(wsum_ps, 1)
            nc.scalar.activation(w_sum[:], ps[:, 3, :], ACT.Copy).then_inc(wsum_ready, 1)
            act.wait_ge(gasum_ps, 1)
            nc.scalar.activation(ga_sum[:], ps[:, 1, 0:GA], ACT.Copy).then_inc(gasum_ready, 1)

            def yhi(t, k):
                act.wait_ge(mixed, t + 1)
                nc.scalar.activation(y_hi[:, k % 2], ps[:, YT + k % 2, :].rearrange("p (c n) -> p c n", c=C),
                                     ACT.Copy).then_inc(yhi_ready, 1)

            def copy_hsT(t, k):
                act.wait_ge(hsT_ps, t + 1)
                nc.scalar.activation(hsT[:, k % 2], ps[:, HT, 0:P], ACT.Copy, scale=2.0).then_inc(hsT_ready, 1)

            yhi(0, 0)
            yhi(1, 1)

            def step(t, k, first, last):
                if not first:
                    copy_hsT(t - 1, (k - 1) % SLOTS)
                act.wait_ge(gap_ready, t + 1)
                nc.scalar.activation(gap_exp[:, k % 2], gap[:, k % 2], ACT.Exp).then_inc(gap_exp_ready, 1)
                if not last:
                    yhi(t + 2, k)

            for k in range(SLOTS):
                step(k, k, k == 0, False)
            with act.Fori(1, GROUPS - 1) as g:
                for k in range(SLOTS):
                    step(g * SLOTS + k, k, False, False)
            for k in range(SLOTS):
                step((GROUPS - 1) * SLOTS + k, k, False, k >= SLOTS - 2)
            copy_hsT(TILES - 1, SLOTS - 1)

        @block.vector
        def _(dve):
            dve.wait_ge(condT_ps, 1)
            nc.vector.tensor_copy(condT[:], ps[:, 0, 0:P]).then_inc(condT_ready, 1)

            def w_lo(c):
                dve.wait_ge(w_hi_ready, c + 1)
                nc.vector.tensor_tensor(wT_lo[:, c, 0:D], ps[:, 4 + c, :], wT_hi[:, c, 0:D].bitcast(f32),
                                        ALU.subtract).then_inc(w_lo_ready, 1)

            w_lo(0)
            w_lo(1)
            dve.wait_ge(logits_ps, 1)
            nc.vector.reduce_max(att_max[:], ps[:, 3, 0:K], AX.X).then_inc(att_step, 1)
            dve.wait_ge(att_step, 1)
            nc.vector.tensor_scalar(att_neg[:], att_max[:], -1.0, None, ALU.mult).then_inc(att_step, 1)
            dve.wait_ge(att_exp_ready, 1)
            nc.vector.reciprocal(att_inv[:], att_sum[:]).then_inc(att_step, 1)
            dve.wait_ge(att_step, 3)
            nc.vector.tensor_scalar(att[:], att_exp[:], att_inv[:], None, ALU.mult).then_inc(att_ready, 1)
            dve.wait_ge(attT_ps, 1)
            nc.vector.tensor_copy(attT[:], ps[0:K, 1, 0:BATCH]).then_inc(attT_ready, 1)
            w_lo(2)
            w_lo(3)
            dve.wait_ge(ga_hi_ready, 1)
            nc.vector.tensor_tensor(wT_lo[:, :, D:WIDE], ps[:, 0, 0:C * GA].rearrange("p (c n) -> p c n", c=C),
                                    wT_hi[:, :, D:WIDE].bitcast(f32), ALU.subtract).then_inc(ga_lo_ready, 1)
            dve.wait_ge(aggb_ps, 1)
            for s in range(SPT):
                rows = slice(s * CH, (s + 1) * CH)
                nc.vector.tensor_copy(agg_b[rows, :], ps[rows, 1, 256:256 + BATCH]
                                      .rearrange("p (t s) -> p s t", s=SPT)[:, s]).then_inc(aggb_ready, 1)
            dve.wait_ge(zeros_ready, 1)
            for r in range(0, ROUNDS, 2):
                dve.wait_ge(agg_ps, r + 1)
                copy_agg(nc.vector.tensor_copy, r, agg_by_dve)
            dve.wait_ge(b_hi_ready, 1)
            nc.vector.tensor_tensor(bT_lo[:], ps[:, 2, :], bT_hi[:].bitcast(f32), ALU.subtract).then_inc(b_lo_ready, 1)
            dve.wait_ge(gasum_ready, 1)
            dve.wait_ge(ones_ready, 4)
            dve.wait_ge(aggb_ready, SPT)

            def ylo(t, k):
                dve.wait_ge(yhi_ready, t + 1)
                nc.vector.tensor_tensor(y_lo[:, k % 2], ps[:, YT + k % 2, :].rearrange("p (c n) -> p c n", c=C),
                                        y_hi[:, k % 2].bitcast(f32), ALU.subtract).then_inc(ylo_ready, 1)

            def link(ins, t, n):
                ins.then_inc(gate_step, 1)
                dve.wait_ge(gate_step, LINKS * t + n)

            def choose(t, k):
                bank, gp = OB + k % 2, k % 2
                scalar = agg_b[:, bass.ds(t, 1)]
                dve.wait_ge(ga_done, t + 1)
                link(nc.vector.scalar_tensor_tensor(
                    out=ga[:, ER:GA], in0=ga_sum[:, ER:GA], scalar=scalar,
                    in1=ps[:, bank, HALF + ER:HALF + GA], op0=ALU.mult, op1=ALU.add), t, 1)
                nc.vector.scalar_tensor_tensor(
                    out=ga[:, 0:ER], in0=ga_sum[:, 0:ER], scalar=scalar,
                    in1=ps[:, bank, HALF:HALF + ER], op0=ALU.mult, op1=ALU.add).then_inc(gate_step, 1)
                link(nc.vector.max(top8[:], ga[:, ER:GA]), t, 3)
                link(nc.vector.tensor_copy(taken[:, 0:2], top8[:, 0:2]), t, 4)
                nc.vector.tensor_scalar(gap[:, gp], ga[:, ER:GA], top8[:, 0:1], None, ALU.subtract).then_inc(gap_ready, 1)
                link(nc.vector.match_replace(rest[:], taken[:], ga[:, ER:GA + 6], LOW), t, 5)
                nc.vector.tensor_tensor(chosen[:], rest[:, 0:E], ga[:, ER:GA], ALU.not_equal).then_inc(gate_step, 1)

            def scale(t, k):
                gp = k % 2
                dve.wait_ge(gate_step, LINKS * t + 6)
                dve.wait_ge(gap_exp_ready, t + 1)
                link(nc.vector.scalar_tensor_tensor(out=gate[:], in0=gap_exp[:, gp], scalar=1.0, in1=chosen[:],
                                                    op0=ALU.mult, op1=ALU.mult, accum_out=gate_total[:]), t, 7)
                link(nc.vector.reciprocal(gate_inv[:], gate_total[:]), t, 8)
                nc.vector.scalar_tensor_tensor(
                    out=hs[:].rearrange("p (e r) -> p e r", e=E), in0=ga[:, 0:ER].rearrange("p (e r) -> p e r", e=E),
                    scalar=gate_inv[:], in1=gate[:].rearrange("p (e a) -> p e a", a=1).to_broadcast([P, E, R]),
                    op0=ALU.mult, op1=ALU.mult).then_inc(hs_step, 1)
                dve.wait_ge(hs_step, 2 * t + 1)
                nc.vector.tensor_copy(hs_parts[:, gp, 0].bitcast(f32r), hs[:]).then_inc(hs_step, 1)
                dve.wait_ge(hs_step, 2 * t + 2)
                nc.vector.tensor_tensor(hs_parts[:, gp, 1], hs[:], hs_parts[:, gp, 0], ALU.subtract).then_inc(hs_ready, 1)

            def finish(t, k, turn, peeled):
                dve.wait_ge(lora_done, t + 1)
                dve.wait_ge(xb_ready, t + 1)
                if not peeled:
                    dve.wait_ge(stored[k], 16 * turn)
                nc.vector.tensor_tensor(o_sb[:, k, HALF:D], ps[:, OB + k % 2, 0:HALF], xb[:, k, HALF:D],
                                        ALU.add).then_inc(half_ready, 1)
                nc.vector.tensor_tensor(o_sb[:, k, 0:HALF], ps[:, OA + k % 2, 0:HALF], xb[:, k, 0:HALF],
                                        ALU.add).then_inc(out_ready, 1)

            ylo(0, 0)
            ylo(1, 1)

            def step(t, k, turn, first, last, peeled):
                choose(t, k)
                if not first:
                    back = 1 if k == 0 else 0
                    finish(t - 1, (k - 1) % SLOTS, turn - back, peeled)
                scale(t, k)
                if not last:
                    ylo(t + 2, k)

            for k in range(SLOTS):
                step(k, k, 0, k == 0, False, True)
            for k in range(SLOTS):
                step(SLOTS + k, k, 1, False, False, k == 0)
            with dve.Fori(2, GROUPS - 1) as g:
                for k in range(SLOTS):
                    step(g * SLOTS + k, k, g, False, False, False)
            for k in range(SLOTS):
                step((GROUPS - 1) * SLOTS + k, k, GROUPS - 1, False, k >= SLOTS - 2, False)
            finish(TILES - 1, SLOTS - 1, GROUPS - 1, False)

        @block.tensor
        def _(pe):
            def transposes_of_w(c):
                for a in range(C):
                    last = nc.tensor.transpose(ps[:, 4 + c, a * P:(a + 1) * P], w_nat[:, a, c * P:(c + 1) * P], ident[:])
                last.then_inc(wT_ps, 1)

            pe.wait_ge(ident_ready, 1)
            pe.wait_ge(cond_in, 16)
            nc.tensor.transpose(ps[:, 0, 0:P], cond_sb[:], ident[:]).then_inc(condT_ps, 1)
            pe.wait_ge(condT_ready, 1)
            pe.wait_ge(w0_in, 32)
            nc.tensor.matmul(ps[:, 1, 0:P], w0_sb[:], condT[:], start=True, stop=True).then_inc(h_ps, 1)
            pe.wait_ge(w_in, 16)
            transposes_of_w(0)
            pe.wait_ge(h_ready, 1)
            pe.wait_ge(w1_in, 32)
            nc.tensor.matmul(ps[:, 2, 0:P], w1_sb[:], h1T[:], start=True, stop=True).then_inc(h_ps, 1)
            transposes_of_w(1)
            pe.wait_ge(h_ready, 2)
            pe.wait_ge(w2_in, 32)
            pe.wait_ge(ones_ready, 2)
            nc.tensor.matmul(ps[:, 3, 0:K], h2T[:], w2_sb[:], start=True, stop=False)
            nc.tensor.matmul(ps[:, 3, 0:K], ones[0:1, :], b2_row[:], start=False, stop=True).then_inc(logits_ps, 1)
            transposes_of_w(2)
            transposes_of_w(3)
            pe.wait_ge(ga_in, 32)
            for c in range(C):
                last = nc.tensor.transpose(ps[:, 0, c * GA:(c + 1) * GA], ga_nat[:, c * P:(c + 1) * P],
                                           ident[0:GA, 0:GA])
            last.then_inc(gaT_ps, 1)
            pe.wait_ge(att_ready, 1)
            nc.tensor.transpose(ps[0:K, 1, 0:BATCH], att[:], ident[:]).then_inc(attT_ps, 1)
            pe.wait_ge(attT_ready, 1)
            pe.wait_ge(mix_in, 16 * SPT)
            pe.wait_ge(mixb_in, 16 * SPT)

            def kernels(o):
                return mix_reps[:, o].rearrange("p s i -> p (s i)")

            nc.tensor.matmul(ps[:, 1, 256:256 + BATCH], kernels(CH), attT[:], start=True, stop=True).then_inc(aggb_ps, 1)
            for r in range(ROUNDS):
                bank = 4 + 2 * (r % 2)
                if r < 2:
                    pe.wait_ge(w_lo_ready, 2 * r + 2)
                else:
                    pe.wait_ge(agg_by_dve if r % 2 == 0 else agg_by_act, SPT * (r // 2))
                for n in range(PER_ROUND):
                    at = (n % (PER_ROUND // 2)) * BATCH
                    last = nc.tensor.matmul(ps[:, bank + n // (PER_ROUND // 2), at:at + BATCH],
                                            kernels(r * PER_ROUND + n), attT[:], start=True, stop=True)
                last.then_inc(agg_ps, 1)
            pe.wait_ge(b_copied, 2)
            for a in range(C):
                last = nc.tensor.transpose(ps[:, 2, a * P:(a + 1) * P], b_twice[:, a].rearrange("p h n -> p (h n)"), ident[:])
            last.then_inc(bT_ps, 1)
            pe.wait_ge(w_lo_ready, C)
            for c in range(C):
                nc.tensor.matmul(ps[:, 3, :], ones_r[:], wT_hi[:, c, 0:D], start=(c == 0), stop=False)
                last = nc.tensor.matmul(ps[:, 3, :], ones_r[:], wT_lo[:, c, 0:D], start=False, stop=(c == C - 1))
            last.then_inc(wsum_ps, 1)
            pe.wait_ge(ga_lo_ready, 1)
            pe.wait_ge(aggb_ready, SPT)
            for c in range(C):
                nc.tensor.matmul(ps[:, 1, 0:GA], ones_r[:], wT_hi[:, c, D:WIDE], start=(c == 0), stop=False)
                last = nc.tensor.matmul(ps[:, 1, 0:GA], ones_r[:], wT_lo[:, c, D:WIDE], start=False, stop=(c == C - 1))
            last.then_inc(gasum_ps, 1)

            def mix(t, k, turn):
                pe.wait_ge(x_in[k], 16 * turn + 16)
                rhs = agg_bd[:].rearrange("p t s o -> p t (s o)")[:, bass.ds(t, 1), :].rearrange("p t n -> p (t n)")
                for c in range(C):
                    last = nc.tensor.matmul(ps[:, YT + k % 2, c * P:(c + 1) * P], x_sb[:, k, c * P:(c + 1) * P],
                                            rhs, start=True, stop=True)
                last.then_inc(mixed, 1)

            def base(t, k, out, cols):
                for c in range(C):
                    hi, lo = y_hi[:, k % 2, c], y_lo[:, k % 2, c]
                    nc.tensor.matmul(out, hi, wT_hi[:, c, cols], start=(c == 0), stop=False)
                    nc.tensor.matmul(out, hi, wT_lo[:, c, cols], start=False, stop=False)
                    last = nc.tensor.matmul(out, lo, wT_hi[:, c, cols], start=False, stop=(c == C - 1))
                return last

            def lora(t, k):
                pe.wait_ge(hsT_ready, t + 1)
                for bank, cols in ((OB, slice(HALF, D)), (OA, slice(0, HALF))):
                    out = ps[:, bank + k % 2, 0:HALF]
                    nc.tensor.matmul(out, hsT[:, k % 2], bT_hi[:, cols], start=False, stop=False, skip_group_check=True)
                    last = nc.tensor.matmul(out, hsT[:, k % 2], bT_lo[:, cols], start=False, stop=True,
                                            skip_group_check=True)
                last.then_inc(lora_done, 1)

            def turn_hs(t, k):
                pe.wait_ge(hs_ready, t + 1)
                nc.tensor.transpose(ps[:, HT, 0:P], hs_parts[:, k % 2].rearrange("p h n -> p (h n)"),
                                    ident[:]).then_inc(hsT_ps, 1)

            def step(t, k, turn, first, last, peeled):
                pe.wait_ge(yhi_ready, t + 1)
                pe.wait_ge(ylo_ready, t + 1)
                if not peeled:
                    pe.wait_ge(half_ready, t - 1)
                base(t, k, ps[:, OB + k % 2, 0:HALF + GA], slice(HALF, WIDE)).then_inc(ga_done, 1)
                if not first:
                    turn_hs(t - 1, (k - 1) % SLOTS)
                if not peeled:
                    pe.wait_ge(out_ready, t - 1)
                base(t, k, ps[:, OA + k % 2, 0:HALF], slice(0, HALF))
                if not first:
                    lora(t - 1, (k - 1) % SLOTS)
                if not last:
                    mix(t + 2, (k + 2) % SLOTS, turn + (1 if k >= SLOTS - 2 else 0))

            pe.wait_ge(agg_by_dve, SPT * (ROUNDS // 2))
            pe.wait_ge(agg_by_act, SPT * (ROUNDS // 2))
            pe.wait_ge(ga_lo_ready, 1)
            mix(0, 0, 0)
            pe.wait_ge(gasum_ready, 1)
            mix(1, 1, 0)
            pe.wait_ge(wsum_ready, 1)
            pe.wait_ge(b_lo_ready, 1)
            for k in range(SLOTS):
                step(k, k, 0, k == 0, False, k < 2)
            with pe.Fori(1, GROUPS - 1) as g:
                for k in range(SLOTS):
                    step(g * SLOTS + k, k, g, False, False, False)
            for k in range(SLOTS):
                step((GROUPS - 1) * SLOTS + k, k, GROUPS - 1, False, k >= SLOTS - 2, False)
            turn_hs(TILES - 1, SLOTS - 1)
            lora(TILES - 1, SLOTS - 1)


_INS = ["x", "cond_128", "L0_cond_W0", "L0_cond_b0", "L0_cond_W1", "L0_cond_b1", "L0_cond_W2", "L0_cond_b2",
        "L0_cond_weight", "L0_cond_bias_k", "L0_ffn_W_base", "L0_ffn_gate_W", "L0_ffn_A", "L0_ffn_B"]


def kernel(**inputs):
    import numpy as _np
    import concourse.bacc as _bacc
    from concourse import mybir as _mybir
    from concourse.bass_utils import run_bass_kernel_spmd as _run

    nc = _bacc.Bacc("TRN2", target_bir_lowering=False, num_devices=1)
    arrays, args = {}, []
    for name in _INS:
        a = _np.ascontiguousarray(inputs[name])
        arrays[f"in_{name}_dram"] = a
        args.append(nc.dram_tensor(f"in_{name}_dram", a.shape, _mybir.dt.from_np(a.dtype), kind="ExternalInput").ap())
    args.append(nc.dram_tensor("out_dram", inputs["x"].shape, _mybir.dt.float32, kind="ExternalOutput").ap())
    adaln_moe_ffn_kernel(nc, *args)
    r = _run(nc, [arrays], core_ids=[0])
    return r.results[0]["out_dram"]
```

```python
import concourse.bass as bass
from concourse import mybir
from contextlib import ExitStack


def adaln_moe_ffn_kernel(nc, x, cond, w0, b0, w1, b1, w2, b2, mix_w, mix_b, w_base, gate_w, lora_a, lora_b, out):
    f32, f32r = mybir.dt.float32, mybir.dt.float32r
    ALU = mybir.AluOpType
    ACT = mybir.ActivationFunctionType
    AX = mybir.AxisListType

    P = 128
    BATCH, CH, D = x.shape
    K = mix_w.shape[0]
    E, R, _ = lora_a.shape
    ER = E * R
    GA = ER + E
    SPT = P // CH
    TILES = BATCH // SPT
    C = D // P
    SLOTS = 4
    GROUPS = TILES // SLOTS
    QUAD = 32
    PARTS = P // QUAD
    HALF = D // 2
    WIDE = D + GA
    LOW = -3.0e38
    OPB = P // CH
    BLOCKS = CH // OPB
    FIRST, OTHERS = slice(0, 2), slice(2, TILES)

    x_tiles = x.rearrange("(t s) c d -> t (s c) d", s=SPT)
    out_tiles = out.rearrange("(t s) c d -> t (s c) d", s=SPT)

    ctx = ExitStack()
    with ctx:
        def sb(name, shape, dt=f32):
            return ctx.enter_context(nc.sbuf_tensor(name, shape, dt))

        def sem(name):
            return ctx.enter_context(nc.semaphore(name))

        ident = sb("ident", [P, P])
        ones = sb("ones", [1, P])
        w_col = sb("w_col", [P, C])
        w_copy = sb("w_copy", [P, C, D])
        ga_col = sb("ga_col", [GA, 1])
        cond_sb = sb("cond_sb", [P, P])
        condT = sb("condT", [P, P])
        w0_sb = sb("w0_sb", [P, P])
        w1_sb = sb("w1_sb", [P, P])
        w2_sb = sb("w2_sb", [P, K])
        b0_col = sb("b0_col", [P, 1])
        b1_col = sb("b1_col", [P, 1])
        b2_row = sb("b2_row", [1, K])
        h1T = sb("h1T", [P, P])
        h2T = sb("h2T", [P, P])
        att_max = sb("att_max", [P, 1])
        att_neg = sb("att_neg", [P, 1])
        att_exp = sb("att_exp", [P, K])
        att_sum = sb("att_sum", [P, 1])
        att_inv = sb("att_inv", [P, 1])
        att = sb("att", [P, K])
        att_parts = sb("att_parts", [P, PARTS, QUAD])
        attT = sb("attT", [P, BATCH], f32r)
        mix_raw = sb("mix_raw", [P, CH + 1, CH])
        mix_parts = sb("mix_parts", [P, CH + 1, CH], f32r)
        warm = sb("warm", [P, 1])
        agg_bd = sb("agg_bd", [P, TILES, SPT, CH])
        agg_b = sb("agg_b", [P, TILES])
        w_nat = sb("w_nat", [P, C, D])
        wT_hi = sb("wT_hi", [P, C, WIDE], f32r)
        wT_lo = sb("wT_lo", [P, C, WIDE], f32r)
        ga_nat = sb("ga_nat", [GA, D])
        b_nat = sb("b_nat", [P, C, ER])
        b_twice = sb("b_twice", [P, C, 2, ER])
        bT_hi = sb("bT_hi", [P, D], f32r)
        bT_lo = sb("bT_lo", [P, D], f32r)
        w_sum = sb("w_sum", [P, D])
        ga_sum = sb("ga_sum", [P, GA])
        x_sb = sb("x_sb", [P, SLOTS, D])
        xb = sb("xb", [P, SLOTS, D])
        xb_part = sb("xb_part", [P, 2, D])
        y_hi = sb("y_hi", [P, 2, C, P], f32r)
        y_lo = sb("y_lo", [P, 2, C, P], f32r)
        ga = sb("ga", [P, GA + 6])
        top8 = sb("top8", [P, 8])
        taken = sb("taken", [P, 8])
        rest = sb("rest", [P, E + 6])
        chosen = sb("chosen", [P, E])
        gap = sb("gap", [P, 2, E])
        gap_exp = sb("gap_exp", [P, 2, E])
        gate = sb("gate", [P, E])
        gate_total = sb("gate_total", [P, 1])
        gate_inv = sb("gate_inv", [P, 1])
        hs = sb("hs", [P, ER])
        hs_parts = sb("hs_parts", [P, 2, 2, ER])
        hsT = sb("hsT", [P, 2, P], f32r)
        o_sb = sb("o_sb", [P, SLOTS, D])

        ps = ctx.enter_context(nc.psum_tensor("ps", [P, 8, 512], f32))
        YT, HT, OA, OB = 0, 2, 4, 6
        WT = (2, 3, 6, 7)

        ident_ready, ones_ready = sem("ident_ready"), sem("ones_ready")
        raw_zeroed, bd_zeroed, warm_ready = sem("raw_zeroed"), sem("bd_zeroed"), sem("warm_ready")
        fill_step = sem("fill_step")
        cond_in, w0_in, w1_in, w2_in = sem("cond_in"), sem("w0_in"), sem("w1_in"), sem("w2_in")
        mixb_in, b0_in, b1_in, b2_in = sem("mixb_in"), sem("b0_in"), sem("b1_in"), sem("b2_in")
        mix_in, ga_in, b_in = sem("mix_in"), sem("ga_in"), sem("b_in")
        w_in = [sem(f"w_in{a}") for a in range(C)]
        mix_hi_ready, mix_parted, mixb_ready = sem("mix_hi_ready"), sem("mix_parted"), sem("mixb_ready")
        condT_ps, condT_ready = sem("condT_ps"), sem("condT_ready")
        h_ps, h_ready = sem("h_ps"), sem("h_ready")
        logits_ps, att_step, att_exp_ready = sem("logits_ps"), sem("att_step"), sem("att_exp_ready")
        att_ready, attT_ps, attT_ready = sem("att_ready"), sem("attT_ps"), sem("attT_ready")
        wT_ps, w_hi_ready, w_lo_ready = sem("wT_ps"), sem("w_hi_ready"), sem("w_lo_ready")
        gaT_ps, ga_hi_ready, ga_lo_ready = sem("gaT_ps"), sem("ga_hi_ready"), sem("ga_lo_ready")
        b_copied, bT_ps, b_hi_ready, b_lo_ready = sem("b_copied"), sem("bT_ps"), sem("b_hi_ready"), sem("b_lo_ready")
        aggT_ps, agg_by_act, agg_by_dve = sem("aggT_ps"), sem("agg_by_act"), sem("agg_by_dve")
        aggb_ps, aggb_ready = sem("aggb_ps"), sem("aggb_ready")
        wcol_ready, wsum_ps, wsum_ready = sem("wcol_ready"), sem("wsum_ps"), sem("wsum_ready")
        gacol_ready, gasum_ps, gasum_ready = sem("gacol_ready"), sem("gasum_ps"), sem("gasum_ready")

        x_in = [sem(f"x_in{k}") for k in range(SLOTS)]
        stored = [sem(f"stored{k}") for k in range(SLOTS)]
        mixed = sem("mixed")
        yhi_ready, ylo_ready = sem("yhi_ready"), sem("ylo_ready")
        ga_done = sem("ga_done")
        gate_step = sem("gate_step")
        gap_ready, gap_exp_ready = sem("gap_ready"), sem("gap_exp_ready")
        hs_ready, hsT_ps, hsT_ready = sem("hs_ready"), sem("hsT_ps"), sem("hsT_ready")
        lora_done, half_ready, out_ready = sem("lora_done"), sem("half_ready"), sem("out_ready")
        xb_step, xb_ready = sem("xb_step"), sem("xb_ready")
        hs_step = sem("hs_step")
        LINKS = 8

        block = ctx.enter_context(nc.Block())

        @block.sync
        def _(sp):
            sp.dma_start(cond_sb[:], cond).then_inc(cond_in, 16)
            sp.dma_start(w0_sb[:], w0).then_inc(w0_in, 16)
            sp.dma_start(w1_sb[:], w1).then_inc(w1_in, 16)
            sp.dma_start(w2_sb[:], w2).then_inc(w2_in, 16)
            sp.wait_ge(raw_zeroed, 1)
            for q in range(PARTS):
                rows = slice(q * QUAD, q * QUAD + K)
                sp.dma_start(mix_raw[rows, 0:CH, :], mix_w.rearrange("k o i a -> k o (i a)")).then_inc(mix_in, 16)
            for a in range(C):
                if a == 2:
                    sp.dma_start(ga_nat[0:ER, :], lora_a.rearrange("e r d -> (e r) d")).then_inc(ga_in, 16)
                    sp.dma_start(ga_nat[ER:GA, :], gate_w).then_inc(ga_in, 16)
                sp.dma_start(w_nat[:, a], w_base[a * P:(a + 1) * P, :]).then_inc(w_in[a], 16)
            for q in range(PARTS):
                sp.dma_start(mix_raw[q * QUAD:q * QUAD + K, CH, :], mix_b).then_inc(mixb_in, 16)
            for k in range(2):
                sp.dma_start(x_sb[:, k], x_tiles[k]).then_inc(x_in[k], 16)
            for a in range(C):
                sp.dma_start(b_nat[:, a].rearrange("p (e r) -> p e r", e=E),
                             lora_b.rearrange("e (a p) r -> a p e r", p=P)[a]).then_inc(b_in, 16)
            for k in range(2, SLOTS):
                sp.dma_start(x_sb[:, k], x_tiles[k]).then_inc(x_in[k], 16)

            def step(t, k, first, last, turn):
                if not first:
                    sp.wait_ge(out_ready, t)
                    sp.dma_start(out_tiles[t - 1], o_sb[:, (k - 1) % SLOTS]).then_inc(stored[(k - 1) % SLOTS], 16)
                if not turn:
                    sp.wait_ge(mixed, t + 1)
                    sp.wait_ge(xb_ready, t + 1)
                    sp.dma_start(x_sb[:, k], x_tiles[t + SLOTS]).then_inc(x_in[k], 16)

            for k in range(SLOTS):
                step(k, k, k == 0, False, False)
            with sp.Fori(1, GROUPS - 1) as g:
                for k in range(SLOTS):
                    step(g * SLOTS + k, k, False, False, False)
            for k in range(SLOTS):
                step((GROUPS - 1) * SLOTS + k, k, False, k == SLOTS - 1, True)
            sp.wait_ge(half_ready, TILES)
            sp.dma_start(out_tiles[TILES - 1][:, HALF:D], o_sb[:, SLOTS - 1, HALF:D]).then_inc(stored[SLOTS - 1], 16)
            sp.wait_ge(out_ready, TILES)
            sp.dma_start(out_tiles[TILES - 1][:, 0:HALF], o_sb[:, SLOTS - 1, 0:HALF]).then_inc(stored[SLOTS - 1], 16)
            for k in range(SLOTS - 1):
                sp.wait_ge(stored[k], 16 * GROUPS)
            sp.wait_ge(stored[SLOTS - 1], 16 * (GROUPS + 1))

        @block.gpsimd
        def _(pool):
            nc.gpsimd.memset(ident[:], 0.0).then_inc(fill_step, 1)
            pool.dma_start(b0_col[:], b0.rearrange("(p a) -> p a", a=1)).then_inc(b0_in, 16)
            pool.wait_ge(fill_step, 1)
            nc.gpsimd.affine_select(out=ident[:], in_=ident[:], compare_op=ALU.not_equal, fill=1.0, base=0,
                                    pattern=[[-1, P]], channel_multiplier=1).then_inc(ident_ready, 1)
            pool.dma_start(b1_col[:], b1.rearrange("(p a) -> p a", a=1)).then_inc(b1_in, 16)
            pool.dma_start(b2_row[:], b2.rearrange("(a k) -> a k", a=1)).then_inc(b2_in, 16)
            nc.gpsimd.memset(ones[:], 1.0).then_inc(ones_ready, 1)
            nc.gpsimd.memset(att_parts[:], 0.0).then_inc(ones_ready, 1)
            half = TILES // 2
            nc.gpsimd.memset(agg_bd[:, half:TILES], 0.0).then_inc(bd_zeroed, 1)
            pool.wait_ge(mixb_in, 16 * PARTS)
            nc.gpsimd.tensor_copy(mix_parts[:, CH], mix_raw[:, CH]).then_inc(fill_step, 1)
            pool.wait_ge(fill_step, 2)
            los = slice(P // 2, P)
            nc.gpsimd.tensor_tensor(mix_parts[los, CH], mix_raw[los, CH], mix_parts[los, CH].bitcast(f32),
                                    ALU.subtract).then_inc(mixb_ready, 1)
            pool.wait_ge(mixb_ready, 1)
            nc.gpsimd.memset(ga[:], LOW).then_inc(ones_ready, 1)
            nc.gpsimd.memset(taken[:], LOW).then_inc(ones_ready, 1)
            pool.wait_ge(b_in, 16 * C)
            nc.gpsimd.tensor_copy(b_twice[:, :, 0], b_nat[:]).then_inc(b_copied, 1)
            nc.gpsimd.tensor_copy(b_twice[:, :, 1], b_nat[:]).then_inc(b_copied, 1)
            pool.wait_ge(wsum_ready, 1)
            pool.wait_ge(aggb_ready, SPT)

            def step(t, k, turn, peeled):
                pool.wait_ge(x_in[k], 16 * turn + 16)
                nc.gpsimd.tensor_tensor(xb_part[:, k % 2], w_sum[:],
                                        agg_b[:, bass.ds(t, 1)].to_broadcast([P, D]), ALU.mult).then_inc(xb_step, 1)
                pool.wait_ge(xb_step, t + 1)
                if not peeled:
                    pool.wait_ge(out_ready, t - SLOTS + 1)
                nc.gpsimd.tensor_tensor(xb[:, k], xb_part[:, k % 2], x_sb[:, k], ALU.add).then_inc(xb_ready, 1)

            for k in range(SLOTS):
                step(k, k, 0, True)
            with pool.Fori(1, GROUPS) as g:
                for k in range(SLOTS):
                    step(g * SLOTS + k, k, g, False)

        def agg_pieces(o, tiles):
            for s in range(SPT):
                src = ps[o * CH:(o + 1) * CH, 4:6, :].rearrange("p a n -> p (a n)") \
                    .rearrange("p (j t s) -> p s t j", s=SPT, t=TILES)[:, s, tiles]
                dst = agg_bd[s * CH:(s + 1) * CH, :, s, :].rearrange("p t (j o) -> p o t j", o=OPB)[:, o, tiles]
                yield dst, src

        @block.scalar
        def _(act):
            act.wait_ge(warm_ready, 1)
            nc.scalar.activation(warm[:], warm[:], ACT.Gelu)

            def w_hi(a):
                act.wait_ge(wT_ps, a + 1)
                nc.scalar.activation(wT_hi[:, :, a * P:(a + 1) * P],
                                     ps[:, WT[a], :].rearrange("p (c n) -> p c n", c=C), ACT.Copy).then_inc(w_hi_ready, 1)

            act.wait_ge(h_ps, 1)
            act.wait_ge(b0_in, 16)
            nc.scalar.activation(h1T[:], ps[:, 0, P:2 * P], ACT.Gelu, bias=b0_col[:]).then_inc(h_ready, 1)
            act.wait_ge(h_ps, 2)
            act.wait_ge(b1_in, 16)
            nc.scalar.activation(h2T[:], ps[:, 0, 2 * P:3 * P], ACT.Gelu, bias=b1_col[:]).then_inc(h_ready, 1)
            act.wait_ge(att_step, 2)
            nc.scalar.activation(att_exp[:], ps[:, 0, 3 * P:3 * P + K], ACT.Exp, bias=att_neg[:],
                                 accum_out=att_sum[:]).then_inc(att_exp_ready, 1)
            w_hi(0)
            w_hi(1)

            def w_row_sums(a):
                act.wait_ge(w_in[a], 16)
                nc.scalar.activation(w_copy[:, a], w_nat[:, a], ACT.Copy,
                                     accum_out=w_col[:, a:a + 1]).then_inc(wcol_ready, 1)

            w_row_sums(0)
            w_row_sums(1)
            w_hi(2)
            act.wait_ge(bd_zeroed, 2)
            act.wait_ge(aggT_ps, 1)

            def spread(tiles):
                for o in (2, 3):
                    for dst, src in agg_pieces(o, tiles):
                        nc.scalar.copy(dst, src).then_inc(agg_by_act, 1)

            spread(FIRST)
            w_hi(3)
            act.wait_ge(aggb_ps, 1)
            for s in range(SPT):
                nc.scalar.copy(agg_b[s * CH:(s + 1) * CH, :], ps[0:CH, 3, 0:BATCH]
                               .rearrange("p (t s) -> p s t", s=SPT)[:, s]).then_inc(aggb_ready, 1)
            act.wait_ge(gaT_ps, 1)
            nc.scalar.activation(wT_hi[:, :, D:WIDE], ps[:, 2, 0:C * GA].rearrange("p (c n) -> p c n", c=C),
                                 ACT.Copy).then_inc(ga_hi_ready, 1)

            def yhi(t, k):
                act.wait_ge(mixed, t + 1)
                nc.scalar.activation(y_hi[:, k % 2], ps[:, YT + k % 2, :].rearrange("p (c n) -> p c n", c=C),
                                     ACT.Copy).then_inc(yhi_ready, 1)

            def copy_hsT(t, k):
                act.wait_ge(hsT_ps, t + 1)
                nc.scalar.activation(hsT[:, k % 2], ps[:, HT, 0:P], ACT.Copy, scale=2.0).then_inc(hsT_ready, 1)

            yhi(0, 0)
            w_row_sums(2)
            w_row_sums(3)
            spread(OTHERS)
            yhi(1, 1)
            act.wait_ge(bT_ps, 1)
            nc.scalar.activation(bT_hi[:], ps[:, 7, :], ACT.Copy).then_inc(b_hi_ready, 1)
            act.wait_ge(gasum_ps, 1)
            nc.scalar.activation(ga_sum[:], ps[:, 2, P:P + GA], ACT.Copy).then_inc(gasum_ready, 1)
            act.wait_ge(wsum_ps, 1)
            nc.scalar.activation(w_sum[:], ps[:, 3, :], ACT.Copy).then_inc(wsum_ready, 1)

            def step(t, k, first, last):
                if not first:
                    copy_hsT(t - 1, (k - 1) % SLOTS)
                act.wait_ge(gap_ready, t + 1)
                nc.scalar.activation(gap_exp[:, k % 2], gap[:, k % 2], ACT.Exp).then_inc(gap_exp_ready, 1)
                if not last:
                    yhi(t + 2, k)

            for k in range(SLOTS):
                step(k, k, k == 0, False)
            with act.Fori(1, GROUPS - 1) as g:
                for k in range(SLOTS):
                    step(g * SLOTS + k, k, False, False)
            for k in range(SLOTS):
                step((GROUPS - 1) * SLOTS + k, k, False, k >= SLOTS - 2)
            copy_hsT(TILES - 1, SLOTS - 1)

        @block.vector
        def _(dve):
            nc.vector.memset(warm[:], 0.0).then_inc(warm_ready, 1)
            nc.vector.memset(mix_raw[:], 0.0).then_inc(raw_zeroed, 1)
            half = TILES // 2
            nc.vector.memset(agg_bd[:, 0:half // 2], 0.0)
            dve.wait_ge(condT_ps, 1)
            nc.vector.tensor_copy(condT[:], ps[:, 0, 0:P]).then_inc(condT_ready, 1)
            nc.vector.memset(agg_bd[:, half // 2:half], 0.0).then_inc(bd_zeroed, 1)

            def w_lo(a):
                dve.wait_ge(w_hi_ready, a + 1)
                cols = slice(a * P, (a + 1) * P)
                nc.vector.tensor_tensor(wT_lo[:, :, cols], ps[:, WT[a], :].rearrange("p (c n) -> p c n", c=C),
                                        wT_hi[:, :, cols].bitcast(f32), ALU.subtract).then_inc(w_lo_ready, 1)

            dve.wait_ge(mix_in, 16 * PARTS)
            nc.vector.tensor_copy(mix_parts[:, 0:CH], mix_raw[:, 0:CH]).then_inc(mix_hi_ready, 1)
            dve.wait_ge(mix_hi_ready, 1)
            los, half = slice(P // 2, P), CH // 2
            nc.vector.tensor_tensor(mix_parts[los, 0:half], mix_raw[los, 0:half], mix_parts[los, 0:half].bitcast(f32),
                                    ALU.subtract).then_inc(mix_parted, 1)
            dve.wait_ge(logits_ps, 1)
            nc.vector.reduce_max(att_max[:], ps[:, 0, 3 * P:3 * P + K], AX.X).then_inc(att_step, 1)
            dve.wait_ge(att_step, 1)
            nc.vector.tensor_scalar(att_neg[:], att_max[:], -1.0, None, ALU.mult).then_inc(att_step, 1)
            nc.vector.tensor_tensor(mix_parts[los, half:CH], mix_raw[los, half:CH], mix_parts[los, half:CH].bitcast(f32),
                                    ALU.subtract).then_inc(mix_parted, 1)
            dve.wait_ge(att_exp_ready, 1)
            nc.vector.reciprocal(att_inv[:], att_sum[:]).then_inc(att_step, 1)
            dve.wait_ge(att_step, 3)
            nc.vector.tensor_scalar(att[:], att_exp[:], att_inv[:], None, ALU.mult).then_inc(att_step, 1)
            dve.wait_ge(att_step, 4)
            dve.wait_ge(ones_ready, 2)
            pairs = att_parts[:].rearrange("p (a h) n -> p a h n", h=2)
            twice = att[:].rearrange("p (a n) -> p a n", a=1).to_broadcast([P, 2, K])
            nc.vector.tensor_copy(pairs[:, :, 0, 0:K].bitcast(f32r), twice).then_inc(att_step, 1)
            dve.wait_ge(att_step, 5)
            nc.vector.tensor_tensor(pairs[:, :, 1, 0:K], twice, pairs[:, :, 0, 0:K], ALU.subtract).then_inc(att_ready, 1)
            dve.wait_ge(ga_in, 32)
            nc.vector.reduce_sum(ga_col[:], ga_nat[:], AX.X).then_inc(gacol_ready, 1)
            dve.wait_ge(attT_ps, 1)
            nc.vector.tensor_copy(attT[:], ps[:, 0, 0:BATCH]).then_inc(attT_ready, 1)
            w_lo(0)
            w_lo(1)
            dve.wait_ge(bd_zeroed, 2)
            dve.wait_ge(aggT_ps, 1)

            def spread(tiles):
                for o in (0, 1):
                    for dst, src in agg_pieces(o, tiles):
                        nc.vector.tensor_copy(dst, src).then_inc(agg_by_dve, 1)

            spread(FIRST)
            w_lo(2)
            w_lo(3)
            dve.wait_ge(ga_hi_ready, 1)
            nc.vector.tensor_tensor(wT_lo[:, :, D:WIDE], ps[:, 2, 0:C * GA].rearrange("p (c n) -> p c n", c=C),
                                    wT_hi[:, :, D:WIDE].bitcast(f32), ALU.subtract).then_inc(ga_lo_ready, 1)

            def ylo(t, k):
                dve.wait_ge(yhi_ready, t + 1)
                nc.vector.tensor_tensor(y_lo[:, k % 2], ps[:, YT + k % 2, :].rearrange("p (c n) -> p c n", c=C),
                                        y_hi[:, k % 2].bitcast(f32), ALU.subtract).then_inc(ylo_ready, 1)

            def link(ins, t, n):
                ins.then_inc(gate_step, 1)
                dve.wait_ge(gate_step, LINKS * t + n)

            def choose(t, k):
                bank, gp = OB + k % 2, k % 2
                scalar = agg_b[:, bass.ds(t, 1)]
                dve.wait_ge(ga_done, t + 1)
                link(nc.vector.scalar_tensor_tensor(
                    out=ga[:, ER:GA], in0=ga_sum[:, ER:GA], scalar=scalar,
                    in1=ps[:, bank, HALF + ER:HALF + GA], op0=ALU.mult, op1=ALU.add), t, 1)
                nc.vector.scalar_tensor_tensor(
                    out=ga[:, 0:ER], in0=ga_sum[:, 0:ER], scalar=scalar,
                    in1=ps[:, bank, HALF:HALF + ER], op0=ALU.mult, op1=ALU.add).then_inc(gate_step, 1)
                link(nc.vector.max(top8[:], ga[:, ER:GA]), t, 3)
                link(nc.vector.tensor_copy(taken[:, 0:2], top8[:, 0:2]), t, 4)
                nc.vector.tensor_scalar(gap[:, gp], ga[:, ER:GA], top8[:, 0:1], None, ALU.subtract).then_inc(gap_ready, 1)
                link(nc.vector.match_replace(rest[:], taken[:], ga[:, ER:GA + 6], LOW), t, 5)
                nc.vector.tensor_tensor(chosen[:], rest[:, 0:E], ga[:, ER:GA], ALU.not_equal).then_inc(gate_step, 1)

            def scale(t, k):
                gp = k % 2
                dve.wait_ge(gate_step, LINKS * t + 6)
                dve.wait_ge(gap_exp_ready, t + 1)
                link(nc.vector.scalar_tensor_tensor(out=gate[:], in0=gap_exp[:, gp], scalar=1.0, in1=chosen[:],
                                                    op0=ALU.mult, op1=ALU.mult, accum_out=gate_total[:]), t, 7)
                link(nc.vector.reciprocal(gate_inv[:], gate_total[:]), t, 8)
                nc.vector.scalar_tensor_tensor(
                    out=hs[:].rearrange("p (e r) -> p e r", e=E), in0=ga[:, 0:ER].rearrange("p (e r) -> p e r", e=E),
                    scalar=gate_inv[:], in1=gate[:].rearrange("p (e a) -> p e a", a=1).to_broadcast([P, E, R]),
                    op0=ALU.mult, op1=ALU.mult).then_inc(hs_step, 1)
                dve.wait_ge(hs_step, 2 * t + 1)
                nc.vector.tensor_copy(hs_parts[:, gp, 0].bitcast(f32r), hs[:]).then_inc(hs_step, 1)
                dve.wait_ge(hs_step, 2 * t + 2)
                nc.vector.tensor_tensor(hs_parts[:, gp, 1], hs[:], hs_parts[:, gp, 0], ALU.subtract).then_inc(hs_ready, 1)

            def finish(t, k, turn, peeled):
                dve.wait_ge(lora_done, 2 * t + 1)
                dve.wait_ge(xb_ready, t + 1)
                if not peeled:
                    dve.wait_ge(stored[k], 16 * turn)
                nc.vector.tensor_tensor(o_sb[:, k, HALF:D], ps[:, OB + k % 2, 0:HALF], xb[:, k, HALF:D],
                                        ALU.add).then_inc(half_ready, 1)
                dve.wait_ge(lora_done, 2 * t + 2)
                nc.vector.tensor_tensor(o_sb[:, k, 0:HALF], ps[:, OA + k % 2, 0:HALF], xb[:, k, 0:HALF],
                                        ALU.add).then_inc(out_ready, 1)

            ylo(0, 0)
            spread(OTHERS)
            ylo(1, 1)
            dve.wait_ge(b_hi_ready, 1)
            nc.vector.tensor_tensor(bT_lo[:], ps[:, 7, :], bT_hi[:].bitcast(f32), ALU.subtract).then_inc(b_lo_ready, 1)
            dve.wait_ge(gasum_ready, 1)
            dve.wait_ge(aggb_ready, SPT)
            dve.wait_ge(ones_ready, 4)

            def step(t, k, turn, first, last, peeled):
                choose(t, k)
                if last and k == SLOTS - 1:
                    scale(t, k)
                if not first:
                    back = 1 if k == 0 else 0
                    finish(t - 1, (k - 1) % SLOTS, turn - back, peeled)
                if not (last and k == SLOTS - 1):
                    scale(t, k)
                if not last:
                    ylo(t + 2, k)

            for k in range(SLOTS):
                step(k, k, 0, k == 0, False, True)
            for k in range(SLOTS):
                step(SLOTS + k, k, 1, False, False, k == 0)
            with dve.Fori(2, GROUPS - 1) as g:
                for k in range(SLOTS):
                    step(g * SLOTS + k, k, g, False, False, False)
            for k in range(SLOTS):
                step((GROUPS - 1) * SLOTS + k, k, GROUPS - 1, False, k >= SLOTS - 2, False)
            finish(TILES - 1, SLOTS - 1, GROUPS - 1, False)

        @block.tensor
        def _(pe):
            def turn_w(a):
                pe.wait_ge(w_in[a], 16)
                for c in range(C):
                    last = nc.tensor.transpose(ps[:, WT[a], c * P:(c + 1) * P], w_nat[:, a, c * P:(c + 1) * P],
                                               ident[:])
                last.then_inc(wT_ps, 1)

            pe.wait_ge(ident_ready, 1)
            pe.wait_ge(cond_in, 16)
            nc.tensor.transpose(ps[:, 0, 0:P], cond_sb[:], ident[:]).then_inc(condT_ps, 1)
            pe.wait_ge(condT_ready, 1)
            pe.wait_ge(w0_in, 16)
            nc.tensor.matmul(ps[:, 0, P:2 * P], w0_sb[:], condT[:], start=True, stop=True).then_inc(h_ps, 1)
            pe.wait_ge(h_ready, 1)
            pe.wait_ge(w1_in, 16)
            nc.tensor.matmul(ps[:, 0, 2 * P:3 * P], w1_sb[:], h1T[:], start=True, stop=True).then_inc(h_ps, 1)
            pe.wait_ge(h_ready, 2)
            pe.wait_ge(w2_in, 16)
            pe.wait_ge(b2_in, 16)
            pe.wait_ge(ones_ready, 1)
            nc.tensor.matmul(ps[:, 0, 3 * P:3 * P + K], h2T[:], w2_sb[:], start=True, stop=False)
            nc.tensor.matmul(ps[:, 0, 3 * P:3 * P + K], ones[:], b2_row[:], start=False,
                             stop=True).then_inc(logits_ps, 1)
            turn_w(0)
            turn_w(1)
            pe.wait_ge(att_ready, 1)
            nc.tensor.transpose(ps[:, 0, 0:BATCH], att_parts[:].rearrange("p a n -> p (a n)"),
                                ident[:]).then_inc(attT_ps, 1)
            turn_w(2)
            pe.wait_ge(attT_ready, 1)
            pe.wait_ge(mix_parted, 2)
            for j in range(BLOCKS):
                last = nc.tensor.matmul(ps[:, 4 + j // 4, (j % 4) * P:(j % 4 + 1) * P],
                                        mix_parts[:, j * OPB:(j + 1) * OPB].rearrange("p o i -> p (o i)"), attT[:],
                                        start=True, stop=True)
            last.then_inc(aggT_ps, 1)
            turn_w(3)
            pe.wait_ge(ga_in, 32)
            pe.wait_ge(w_lo_ready, 1)
            for c in range(C):
                last = nc.tensor.transpose(ps[:, 2, c * GA:(c + 1) * GA], ga_nat[:, c * P:(c + 1) * P],
                                           ident[0:GA, 0:GA])
            last.then_inc(gaT_ps, 1)
            pe.wait_ge(mixb_ready, 1)
            pe.wait_ge(w_lo_ready, 2)
            nc.tensor.matmul(ps[0:CH, 3, 0:BATCH], mix_parts[:, CH], attT[:],
                             start=True, stop=True).then_inc(aggb_ps, 1)

            def mix(t, k, turn):
                pe.wait_ge(x_in[k], 16 * turn + 16)
                rhs = agg_bd[:].rearrange("p t s o -> p t (s o)")[:, bass.ds(t, 1), :].rearrange("p t n -> p (t n)")
                for c in range(C):
                    last = nc.tensor.matmul(ps[:, YT + k % 2, c * P:(c + 1) * P], x_sb[:, k, c * P:(c + 1) * P],
                                            rhs, start=True, stop=True)
                last.then_inc(mixed, 1)

            def base(t, k, out, cols, terms=range(3)):
                for term in terms:
                    if term == 2:
                        pe.wait_ge(ylo_ready, t + 1)
                    y, w = (y_lo if term == 2 else y_hi), (wT_lo if term == 1 else wT_hi)
                    for c in range(C):
                        last = nc.tensor.matmul(out, y[:, k % 2, c], w[:, c, cols], start=(term == 0 and c == 0),
                                                stop=(term == 2 and c == C - 1))
                return last

            def lora(t, k):
                pe.wait_ge(hsT_ready, t + 1)
                for bank, cols in ((OB, slice(HALF, D)), (OA, slice(0, HALF))):
                    out = ps[:, bank + k % 2, 0:HALF]
                    nc.tensor.matmul(out, hsT[:, k % 2], bT_hi[:, cols], start=False, stop=False, skip_group_check=True)
                    nc.tensor.matmul(out, hsT[:, k % 2], bT_lo[:, cols], start=False, stop=True,
                                     skip_group_check=True).then_inc(lora_done, 1)

            def turn_hs(t, k):
                pe.wait_ge(hs_ready, t + 1)
                nc.tensor.transpose(ps[:, HT, 0:P], hs_parts[:, k % 2].rearrange("p h n -> p (h n)"),
                                    ident[:]).then_inc(hsT_ps, 1)

            def turn_b():
                pe.wait_ge(b_copied, 2)
                for a in range(C):
                    last = nc.tensor.transpose(ps[:, 7, a * P:(a + 1) * P],
                                               b_twice[:, a].rearrange("p h n -> p (h n)"), ident[:])
                last.then_inc(bT_ps, 1)

            def sums():
                pe.wait_ge(gacol_ready, 1)
                nc.tensor.matmul(ps[:, 2, P:P + GA], ga_col[:].to_broadcast([GA, P]), ident[0:GA, 0:GA],
                                 start=True, stop=True).then_inc(gasum_ps, 1)
                pe.wait_ge(wcol_ready, C)
                pe.wait_ge(aggb_ready, SPT)
                for a in range(C):
                    last = nc.tensor.matmul(ps[:, 3, a * P:(a + 1) * P], w_col[:, a:a + 1].to_broadcast([P, P]),
                                            ident[:], start=True, stop=True)
                last.then_inc(wsum_ps, 1)

            def step(t, k, turn, first, last, peeled):
                if first:
                    pe.wait_ge(w_lo_ready, C)
                    pe.wait_ge(ga_lo_ready, 1)
                pe.wait_ge(yhi_ready, t + 1)
                if peeled and not first:
                    pe.wait_ge(b_lo_ready, 1)
                if not peeled:
                    pe.wait_ge(half_ready, t - 1)
                base(t, k, ps[:, OB + k % 2, 0:HALF + GA], slice(HALF, WIDE)).then_inc(ga_done, 1)
                if first:
                    sums()
                    turn_b()
                    pe.wait_ge(agg_by_act, 4 * SPT)
                    pe.wait_ge(agg_by_dve, 4 * SPT)
                else:
                    turn_hs(t - 1, (k - 1) % SLOTS)
                if not peeled:
                    pe.wait_ge(out_ready, t - 1)
                out, cols = ps[:, OA + k % 2, 0:HALF], slice(0, HALF)
                split = 1 if last else 2
                base(t, k, out, cols, range(split))
                if not first:
                    lora(t - 1, (k - 1) % SLOTS)
                base(t, k, out, cols, range(split, 3))
                if not last:
                    mix(t + 2, (k + 2) % SLOTS, turn + (1 if k >= SLOTS - 2 else 0))

            pe.wait_ge(agg_by_act, 2 * SPT)
            pe.wait_ge(agg_by_dve, 2 * SPT)
            mix(0, 0, 0)
            mix(1, 1, 0)
            for k in range(SLOTS):
                step(k, k, 0, k == 0, False, k < 2)
            with pe.Fori(1, GROUPS - 1) as g:
                for k in range(SLOTS):
                    step(g * SLOTS + k, k, g, False, False, False)
            for k in range(SLOTS):
                step((GROUPS - 1) * SLOTS + k, k, GROUPS - 1, False, k >= SLOTS - 2, False)
            turn_hs(TILES - 1, SLOTS - 1)
            lora(TILES - 1, SLOTS - 1)


_INS = ["x", "cond_128", "L0_cond_W0", "L0_cond_b0", "L0_cond_W1", "L0_cond_b1", "L0_cond_W2", "L0_cond_b2",
        "L0_cond_weight", "L0_cond_bias_k", "L0_ffn_W_base", "L0_ffn_gate_W", "L0_ffn_A", "L0_ffn_B"]


def kernel(**inputs):
    import numpy as _np
    import concourse.bacc as _bacc
    from concourse import mybir as _mybir
    from concourse.bass_utils import run_bass_kernel_spmd as _run

    nc = _bacc.Bacc("TRN2", target_bir_lowering=False, num_devices=1)
    arrays, args = {}, []
    for name in _INS:
        a = _np.ascontiguousarray(inputs[name])
        arrays[f"in_{name}_dram"] = a
        args.append(nc.dram_tensor(f"in_{name}_dram", a.shape, _mybir.dt.from_np(a.dtype), kind="ExternalInput").ap())
    args.append(nc.dram_tensor("out_dram", inputs["x"].shape, _mybir.dt.float32, kind="ExternalOutput").ap())
    adaln_moe_ffn_kernel(nc, *args)
    r = _run(nc, [arrays], core_ids=[0])
    return r.results[0]["out_dram"]
```
